# Optimizing a Trainium2 kernel written in Bass

```python
import numpy as np
import jax
import jax.numpy as jnp

def _softmax(x, axis=-1):
    return jax.nn.softmax(x, axis=axis)

def _gelu(x):
    return jax.nn.gelu(x, approximate=True)

def _silu(x):
    return jax.nn.silu(x)

def _sigmoid(x):
    return jax.nn.sigmoid(x)

def _layernorm(x, axis=-1, eps=1e-05):
    m = jnp.mean(x, axis=axis, keepdims=True)
    v = jnp.var(x, axis=axis, keepdims=True)
    return (x - m) / jnp.sqrt(v + eps)

def _scatter_add(tgt, idx, src, axis=0):
    return tgt.at[idx].add(src)

def _segment_sum(src, seg, n):
    return jax.ops.segment_sum(src, seg, n)
kernel_name = 'mk_seq_preln_d1_jaxref_r4_dba53b'

def setup_inputs(seed: int=0):
    np.random.seed(seed)
    _w = jnp.asarray

    def _L0_attn_setup():
        import jax, jax.numpy as jnp
        import numpy as np
        H = 256
        NH = 16
        HD = H // NH

        def rotate_half(x):
            x1, x2 = jnp.split(x, 2, axis=-1)
            return jnp.concatenate((-x2, x1), axis=-1)

        def apply_rope(q, k, cos, sin):
            q = q.astype(jnp.bfloat16)
            k = k.astype(jnp.bfloat16)
            cos = cos.astype(jnp.bfloat16)[None, None]
            sin = sin.astype(jnp.bfloat16)[None, None]
            n_prefix = q.shape[-2] - cos.shape[-2]
            q_pre, q_pat = jnp.split(q, [n_prefix], axis=-2)
            k_pre, k_pat = jnp.split(k, [n_prefix], axis=-2)
            q_pat = q_pat * cos + rotate_half(q_pat) * sin
            k_pat = k_pat * cos + rotate_half(k_pat) * sin
            q = jnp.concatenate([q_pre, q_pat], axis=-2).astype(jnp.float32)
            k = jnp.concatenate([k_pre, k_pat], axis=-2).astype(jnp.float32)
            return (q, k)
        key = jax.random.key(seed)
        ks = jax.random.split(key, 12)
        B, T, P = (16, 1029, 256)
        s = 1.0 / np.sqrt(H)
        return {'hidden_states': jax.random.normal(ks[0], (B, T, H), dtype=jnp.float32), 'cos': jax.random.uniform(ks[1], (P, HD), dtype=jnp.float32, minval=-1.0, maxval=1.0), 'sin': jax.random.uniform(ks[2], (P, HD), dtype=jnp.float32, minval=-1.0, maxval=1.0), 'wq': jax.random.normal(ks[3], (H, H), dtype=jnp.float32) * s, 'bq': jax.random.normal(ks[4], (H,), dtype=jnp.float32) * 0.01, 'wk': jax.random.normal(ks[5], (H, H), dtype=jnp.float32) * s, 'wv': jax.random.normal(ks[6], (H, H), dtype=jnp.float32) * s, 'bv': jax.random.normal(ks[7], (H,), dtype=jnp.float32) * 0.01, 'wo': jax.random.normal(ks[8], (H, H), dtype=jnp.float32) * s, 'bo': jax.random.normal(ks[9], (H,), dtype=jnp.float32) * 0.01}
    _L0_attn_in = _L0_attn_setup()

    def _L0_ffn_setup():
        import jax, jax.numpy as jnp
        import numpy as np
        B, S, D = (4, 1024, 256)
        E, F_EXP = (16, 512)
        F_C = 2.0
        F_SH = 512
        key = jax.random.key(seed)
        ks = jax.random.split(key, 8)
        s = 0.02
        return {'hidden_states': jax.random.normal(ks[0], (B, S, D), jnp.float32), 'gate_w': jax.random.normal(ks[1], (E, D), jnp.float32) * s, 'Wg': jax.random.normal(ks[2], (E, F_EXP, D), jnp.float32) * s, 'Wu': jax.random.normal(ks[3], (E, F_EXP, D), jnp.float32) * s, 'Wd': jax.random.normal(ks[4], (E, D, F_EXP), jnp.float32) * s, 'Ws_g': jax.random.normal(ks[5], (F_SH, D), jnp.float32) * s, 'Ws_u': jax.random.normal(ks[6], (F_SH, D), jnp.float32) * s, 'Ws_d': jax.random.normal(ks[7], (D, F_SH), jnp.float32) * s}
    _L0_ffn_in = _L0_ffn_setup()
    _d = {'L0_attn_hidden_states': _L0_attn_in['hidden_states'], 'L0_attn_cos': _L0_attn_in['cos'], 'L0_attn_sin': _L0_attn_in['sin'], 'L0_attn_wq': _L0_attn_in['wq'], 'L0_attn_bq': _L0_attn_in['bq'], 'L0_attn_wk': _L0_attn_in['wk'], 'L0_attn_wv': _L0_attn_in['wv'], 'L0_attn_bv': _L0_attn_in['bv'], 'L0_attn_wo': _L0_attn_in['wo'], 'L0_attn_bo': _L0_attn_in['bo'], 'L0_ffn_gate_w': _L0_ffn_in['gate_w'], 'L0_ffn_Wg': _L0_ffn_in['Wg'], 'L0_ffn_Wu': _L0_ffn_in['Wu'], 'L0_ffn_Wd': _L0_ffn_in['Wd'], 'L0_ffn_Ws_g': _L0_ffn_in['Ws_g'], 'L0_ffn_Ws_u': _L0_ffn_in['Ws_u'], 'L0_ffn_Ws_d': _L0_ffn_in['Ws_d']}
    _x0 = _d['L0_attn_hidden_states']
    _d['L0_attn_hidden_states'] = jax.random.normal(jax.random.fold_in(jax.random.key(seed), 1), (8, 1024, 256), dtype=_x0.dtype)
    del _x0
    return _d

def reference(L0_attn_hidden_states, L0_attn_cos, L0_attn_sin, L0_attn_wq, L0_attn_bq, L0_attn_wk, L0_attn_wv, L0_attn_bv, L0_attn_wo, L0_attn_bo, L0_ffn_gate_w, L0_ffn_Wg, L0_ffn_Wu, L0_ffn_Wd, L0_ffn_Ws_g, L0_ffn_Ws_u, L0_ffn_Ws_d):

    def _L0_attn_ref(hidden_states, cos, sin, wq, bq, wk, wv, bv, wo, bo):
        import jax, jax.numpy as jnp
        import numpy as np
        H = 256
        NH = 16
        HD = H // NH

        def rotate_half(x):
            x1, x2 = jnp.split(x, 2, axis=-1)
            return jnp.concatenate((-x2, x1), axis=-1)

        def apply_rope(q, k, cos, sin):
            q = q.astype(jnp.bfloat16)
            k = k.astype(jnp.bfloat16)
            cos = cos.astype(jnp.bfloat16)[None, None]
            sin = sin.astype(jnp.bfloat16)[None, None]
            n_prefix = q.shape[-2] - cos.shape[-2]
            q_pre, q_pat = jnp.split(q, [n_prefix], axis=-2)
            k_pre, k_pat = jnp.split(k, [n_prefix], axis=-2)
            q_pat = q_pat * cos + rotate_half(q_pat) * sin
            k_pat = k_pat * cos + rotate_half(k_pat) * sin
            q = jnp.concatenate([q_pre, q_pat], axis=-2).astype(jnp.float32)
            k = jnp.concatenate([k_pre, k_pat], axis=-2).astype(jnp.float32)
            return (q, k)
        B, T, _ = hidden_states.shape
        q = (hidden_states @ wq + bq).reshape(B, T, NH, HD).transpose(0, 2, 1, 3)
        k = (hidden_states @ wk).reshape(B, T, NH, HD).transpose(0, 2, 1, 3)
        v = (hidden_states @ wv + bv).reshape(B, T, NH, HD).transpose(0, 2, 1, 3)
        q, k = apply_rope(q, k, cos, sin)
        scale = 1.0 / jnp.sqrt(jnp.float32(HD))
        scores = jnp.einsum('bhqd,bhkd->bhqk', q, k) * scale
        attn = jax.nn.softmax(scores, axis=-1)
        out = jnp.einsum('bhqk,bhkd->bhqd', attn, v)
        out = out.transpose(0, 2, 1, 3).reshape(B, T, H)
        return out @ wo + bo

    def _L0_ffn_ref(hidden_states, gate_w, Wg, Wu, Wd, Ws_g, Ws_u, Ws_d):
        import jax, jax.numpy as jnp
        import numpy as np
        B, S, D = (4, 1024, 256)
        E, F_EXP = (16, 512)
        F_C = 2.0
        F_SH = 512
        b, s, d = hidden_states.shape
        e = gate_w.shape[0]
        cap = int(s * F_C / e)
        logits = jnp.einsum('bsd,ed->bse', hidden_states, gate_w)
        scores = jax.nn.softmax(logits, axis=-1).transpose(0, 2, 1)
        topk_w, topk_idx = jax.lax.top_k(scores, cap)
        x_tok = jnp.take_along_axis(hidden_states[:, None, :, :], topk_idx[..., None], axis=2)
        g = jnp.einsum('becd,efd->becf', x_tok, Wg)
        u = jnp.einsum('becd,efd->becf', x_tok, Wu)
        h = jax.nn.gelu(g, approximate=False) * u
        eo = jnp.einsum('becf,edf->becd', h, Wd) * topk_w[..., None]
        offs = (jnp.arange(b) * s)[:, None, None]
        flat_idx = (topk_idx + offs).reshape(-1)
        flat = jnp.zeros((b * s, d), hidden_states.dtype)
        flat = flat.at[flat_idx].add(eo.reshape(-1, d))
        out = flat.reshape(b, s, d)
        gs = jnp.einsum('bsd,fd->bsf', hidden_states, Ws_g)
        us = jnp.einsum('bsd,fd->bsf', hidden_states, Ws_u)
        shared = jnp.einsum('bsf,df->bsd', jax.nn.gelu(gs, approximate=False) * us, Ws_d)
        return out + shared
    x = L0_attn_hidden_states
    x = x + _L0_attn_ref(_layernorm(x, axis=-1), L0_attn_cos, L0_attn_sin, L0_attn_wq, L0_attn_bq, L0_attn_wk, L0_attn_wv, L0_attn_bv, L0_attn_wo, L0_attn_bo)
    x = x + _L0_ffn_ref(_layernorm(x, axis=-1), L0_ffn_gate_w, L0_ffn_Wg, L0_ffn_Wu, L0_ffn_Wd, L0_ffn_Ws_g, L0_ffn_Ws_u, L0_ffn_Ws_d)
    return x

_drawn_inputs = setup_inputs


def setup_inputs(seed=0):
    import zlib

    import numpy as np

    out = dict(_drawn_inputs(seed))
    spreads = {}
    factors = {'L0_attn_bq': 32.985,
     'L0_attn_bv': 5.825,
     'L0_attn_bo': 5.496,
     'L0_ffn_gate_w': 8.0,
     'L0_ffn_Wg': 8.0,
     'L0_ffn_Wu': 8.0,
     'L0_ffn_Wd': 8.0,
     'L0_ffn_Ws_g': 8.0,
     'L0_ffn_Ws_u': 8.0,
     'L0_ffn_Ws_d': 8.0}
    for name, (base, spread) in spreads.items():
        noise = np.random.default_rng([zlib.crc32(name.encode()), seed]).standard_normal(out[name].shape)
        drawn = base * np.exp(spread * noise) if base else spread * noise
        out[name] = jnp.asarray(drawn.astype(out[name].dtype))
    for name, factor in factors.items():
        out[name] = (out[name] * factor).astype(out[name].dtype)
    return out
```

```python
import concourse.bass as bass
from concourse import mybir
from contextlib import ExitStack

F32 = mybir.dt.float32
BF16 = mybir.dt.bfloat16
I32 = mybir.dt.int32
U32 = mybir.dt.uint32
ALU = mybir.AluOpType
ACT = mybir.ActivationFunctionType
AX = mybir.AxisListType

P = 128
QUAD = 32
EPS = 1e-5
NEWTON_STEPS = 4
RSQRT_MAGIC = float(0x5F3759DF)


class Tally:

    def __init__(self, sem, base=0):
        self.sem, self.base, self.n = sem, base, 0

    def inc(self, instruction):
        instruction.then_inc(self.sem, 1)
        self.n += 1

    def wait(self, engine):
        engine.wait_ge(self.sem, self.base + self.n)


def rsqrt_steps(nc, dve, own, y, tmp, half, var):
    own.inc(nc.vector.tensor_scalar(tmp, var, EPS, None, ALU.add))
    own.wait(dve)
    own.inc(nc.vector.tensor_scalar(half, tmp, -0.5, None, ALU.mult))
    own.inc(nc.vector.tensor_scalar(y.bitcast(I32), tmp.bitcast(I32), 1, None, ALU.logical_shift_right))
    own.wait(dve)
    own.inc(nc.vector.tensor_scalar(y.bitcast(I32), y.bitcast(I32), -1.0, RSQRT_MAGIC, ALU.mult, ALU.add))
    for n in range(NEWTON_STEPS):
        own.wait(dve)
        own.inc(nc.vector.tensor_tensor(tmp, y, y, ALU.mult))
        own.wait(dve)
        own.inc(nc.vector.tensor_tensor(tmp, tmp, half, ALU.mult))
        own.wait(dve)
        last = nc.vector.scalar_tensor_tensor(y, tmp, 1.5, y, ALU.add, ALU.mult)
        if n < NEWTON_STEPS - 1:
            own.inc(last)
    return last


RSQRT_INCS = 3 + 3 * NEWTON_STEPS


def attention(nc, d, X, B):
    H, NH, HD = 256, 16, 16
    T = 1024
    TT = T // P
    G = NH // 4
    KH = H // P
    NQ = T // 512
    STEPS = NQ * TT
    ROPE_TILES = 2
    SC = 4 * TT
    LEAD = 10
    ST_BANKS = 3
    P_STEPS = 2

    def scores(grp, a, z):
        return [("sc", grp, n // TT, n % TT) for n in range(a, z)]

    def slot_items(g, last):
        t = g + 1
        base = scores(t, LEAD, SC) + scores(t + 1, 0, 4) + [("nm", t)] + scores(t + 1, 4, LEAD)
        steps = [[] for _ in range(STEPS)]
        for n, item in enumerate(base):
            steps[n * STEPS // len(base)].append(item)
        extra = {11: [("ot", g, 0)]}
        if g:
            extra[3] = [("ot", g - 1, 1)]
        if g == 0:
            extra[1] = [("qkT", 2)]
        if g == 1:
            extra |= {1: [("qkT", 3)], 2: [("xt", 0, 1)], 4: [("xt", 1, 1)],
                      6: [("qk", 0, 1)], 8: [("qk", 1, 1)], 10: [("qk", 2, 1)], 13: [("qk", 3, 1)]}
        if g == 2:
            extra[5] = [("qkT", G)]
        if g == 3:
            extra[1] = [("qkT", G + 1)]
        for s, items in extra.items():
            steps[s] = items + steps[s]
        if last:
            steps = [[i for i in st if not (i[0] in ("xt", "qk") or (i[0] in ("sc", "nm", "qkT") and i[1] >= G))]
                     for st in steps]
        return steps

    def schedule(last):
        slots = [slot_items(g, last) for g in range(G)]
        flush = [("ot", G - 1, 1), ("aot", 0), ("aot", 1), ("proj", 0), ("proj", 1)]
        if not last:
            flush += [("v", 0), ("v", 1)]
        order = [i for sl in slots for st in sl for i in st] + flush
        return slots, flush, {item: n for n, item in enumerate(order)}, len(order)

    PRO = ([("xt", 0, 0), ("xt", 1, 0)] + [("qk", n, 0) for n in range(4)] + [("qkT", 0), ("qkT", 1), ("v", 0), ("v", 1)]
           + scores(0, 0, SC) + scores(1, 0, 4) + [("nm", 0)] + scores(1, 4, LEAD))
    PRO_ORD = {item: n for n, item in enumerate(PRO)}
    NPRO = len(PRO)
    _, _, _, NLOOP = schedule(False)
    assert NLOOP % 2 == 0

    ctx = ExitStack()
    with ctx:
        def sb(name, shape, dt):
            return ctx.enter_context(nc.sbuf_tensor("sb_" + name, shape, dt))

        def sem(name):
            return ctx.enter_context(nc.semaphore(name))

        ident = sb("ident", [P, P], F32)
        identb = sb("identb", [P, P], BF16)
        w_qk = sb("w_qk", [P, KH, 2 * H], F32)
        w_v = sb("w_v", [P, KH, H], F32)
        w_o = sb("w_o", [P, KH, H], F32)
        b_q = sb("b_q", [P, H], F32)
        b_v = sb("b_v", [P, H], F32)
        b_o = sb("b_o", [P, H], F32)
        cs_in = sb("cs_in", [P, 2, ROPE_TILES, HD], F32)
        cosb = sb("cosb", [P, ROPE_TILES, HD], BF16)
        sinb = sb("sinb", [P, ROPE_TILES, HD], BF16)
        XN = sb("XN", [P, TT, H], F32)
        AOT = XN[:, :, :].rearrange("p a c -> p (a c)").rearrange("p (k n) -> p k n", k=KH)
        XNT = sb("XNT", [P, KH, T], F32)
        QP = sb("QP", [P, TT, NH, QUAD], BF16)
        KP = sb("KP", [P, TT, NH, QUAD], BF16)
        QS = sb("QS", [P, T], BF16)
        KT = [sb(f"KT{g}", [P, T], BF16) for g in range(G)]
        QM = [[sb(f"QM{g}{j}", [P, T], BF16) for j in range(4)] for g in range(G)]
        VA = sb("VA", [P, TT, NH, QUAD], F32)
        PR = [sb(f"PR{n}", [P, 4, 512], F32) for n in range(P_STEPS)]
        OT = sb("OT", [P, 512], F32)
        AO = sb("AO", [P, TT, H], F32)
        NS = sb("NS", [12, T], BF16)
        MX = sb("MX", [P, 2, 4, TT], F32)
        NM = sb("NM", [P, TT, 4, 3], BF16)
        nmr = sb("nmr", [P, 4, TT], F32)
        RD = sb("RD", [P, 2, 4, 4], F32)
        stats = sb("stats", [P, TT, 6], F32)
        mv = sb("mv", [P, TT, 2], F32)
        rstd = sb("rstd", [P, TT], F32)
        nt1 = sb("nt1", [P, TT], F32)
        nt2 = sb("nt2", [P, TT], F32)
        rt1 = sb("rt1", [P, ROPE_TILES, NH, HD], BF16)
        rt2 = sb("rt2", [P, ROPE_TILES, NH, HD], BF16)
        credit = sb("credit", [P, 2], F32)
        dve_scratch = sb("dve_scratch", [P, 1], F32)
        pool_scratch = sb("pool_scratch", [P, 1], F32)

        ring = [ctx.enter_context(nc.psum_tensor(f"ring{i}", [P, 2, 512], F32)) for i in range(2)]
        st_bank = [ctx.enter_context(nc.psum_tensor(f"st{i}", [P, 512], F32)) for i in range(ST_BANKS)]
        pv_bank = ctx.enter_context(nc.psum_tensor("pv", [P, 512], F32))

        const_in = sem("const_in")
        x_in = sem("x_in")
        const_ready = sem("const_ready")
        fills = sem("fills")
        bias_added = sem("bias_added")
        xn_ready = sem("xn_ready")
        ring_full = sem("ring_full")
        ring_free = sem("ring_free")
        rope_done = sem("rope_done")
        qm_in = sem("qm_in")
        nm_ready = sem("nm_ready")
        nm_in = sem("nm_in")
        st_full = sem("st_full")
        st_free = sem("st_free")
        pv_done = sem("pv_done")
        ot_ready = sem("ot_ready")
        dve_own = sem("dve_own")
        pool_own = sem("pool_own")

        N_CONST = 9

        def ring_base(b):
            return NPRO + b * NLOOP

        block = ctx.enter_context(nc.Block())

        @block.sync
        def _(sp):
            sp.dma_start(X[:, 0:TT, :], d["x"][0:T, :].rearrange("(i p) h -> p i h", p=P)).then_inc(x_in, 16)
            sp.dma_start(ident[:], d["ident"]).then_inc(const_in, 16)
            sp.dma_start(w_qk[:, :, 0:H], d["wq"].rearrange("(k p) n -> p k n", p=P)).then_inc(const_in, 16)
            sp.dma_start(w_qk[:, :, H:2 * H], d["wk"].rearrange("(k p) n -> p k n", p=P)).then_inc(const_in, 16)
            sp.dma_start(w_v[:], d["wv"].rearrange("(k p) n -> p k n", p=P)).then_inc(const_in, 16)
            sp.dma_start(w_o[:], d["wo"].rearrange("(k p) n -> p k n", p=P)).then_inc(const_in, 16)
            sp.dma_start(b_q[:], d["bq"].partition_broadcast(P)).then_inc(const_in, 16)
            sp.dma_start(b_v[:], d["bv"].partition_broadcast(P)).then_inc(const_in, 16)
            sp.dma_start(b_o[:], d["bo"].partition_broadcast(P)).then_inc(const_in, 16)
            sp.dma_start(cs_in[:, 0], d["cos"].rearrange("(i p) h -> p i h", p=P)).then_inc(const_in, 16)
            sp.dma_start(cs_in[:, 1], d["sin"].rearrange("(i p) h -> p i h", p=P)).then_inc(const_in, 16)

            def load_heads(grp, after):
                sp.wait_ge(ring_free, after)
                for j in range(4):
                    r = slice(QUAD * j, QUAD * j + QUAD)
                    sp.dma_start(QM[grp % G][j][r, :], QS[r, :]).then_inc(qm_in, 16)

            def load_maxima(grp, after):
                sp.wait_ge(ring_free, after)
                for j in range(4):
                    sp.dma_start(QM[grp % G][j][QUAD * j + HD:QUAD * j + HD + 3, :],
                                 NS[3 * j:3 * j + 3, :]).then_inc(nm_in, 16)

            sp.wait_ge(fills, 4 * G)
            load_heads(0, PRO_ORD["qkT", 0] + 1)
            load_heads(1, PRO_ORD["qkT", 1] + 1)
            load_maxima(0, PRO_ORD["nm", 0] + 1)

            def batch(b, last):
                if not last:
                    sp.wait_ge(x_in, 16 * (b + 1))
                    sp.dma_start(X[:, bass.ds((b + 1) * TT, TT), :],
                                 d["x"][bass.ds((b + 1) * T, T), :].rearrange("(i p) h -> p i h", p=P)
                                 ).then_inc(x_in, 16)
                slots, _, order, _ = schedule(last)
                for steps in slots:
                    for item in [i for st in steps for i in st]:
                        if item[0] == "qkT":
                            load_heads(item[1], ring_base(b) + order[item] + 1)
                        if item[0] == "nm":
                            load_maxima(item[1], ring_base(b) + order[item] + 1)

            if B > 1:
                with sp.Fori(0, B - 1) as b:
                    batch(b, False)
            batch(B - 1, True)
            sp.wait_ge(x_in, 16 * B)
            sp.wait_ge(nm_in, 64 * G * B)

        @block.gpsimd
        def _(pool):
            own = Tally(pool_own)
            for tiles in QM:
                for t in tiles:
                    nc.gpsimd.memset(t[:], 0.0).then_inc(fills, 1)

            def settle():
                nc.gpsimd.tensor_tensor(pool_scratch[:], ident[:, 0:1], ident[:, 0:1], ALU.mult)

            def add_bias(b):
                pool.wait_ge(xn_ready, TT * (b + 1))
                for i in range(TT):
                    nc.gpsimd.tensor_tensor(X[:, b * TT + i, :], X[:, b * TT + i, :], b_o[:],
                                            ALU.add).then_inc(bias_added, 1)

            def rope(b, own, after):
                pool.wait_ge(ring_free, after)
                for n, A in enumerate((QP, KP)):
                    if n:
                        pool.wait_ge(rope_done, 2 * b + 1)
                    a = A[:, TT - ROPE_TILES:TT, :, 0:HD]
                    h = HD // 2

                    def over(c, lo, hi):
                        return c[:, :, lo:hi].unsqueeze(2).to_broadcast([P, ROPE_TILES, NH, hi - lo])
                    nc.gpsimd.tensor_tensor(rt1[:], a, over(cosb, 0, HD), ALU.mult)
                    nc.gpsimd.tensor_tensor(rt2[:, :, :, 0:h], a[:, :, :, h:HD], over(sinb, 0, h), ALU.mult)
                    own.inc(nc.gpsimd.tensor_tensor(rt2[:, :, :, h:HD], a[:, :, :, 0:h], over(sinb, h, HD), ALU.mult))
                    own.wait(pool)
                    nc.gpsimd.tensor_tensor(a, rt1[:], rt2[:], ALU.add).then_inc(rope_done, 1)

            ROPE_INCS = 2

            def negated_maxima(grp, own, after):
                pool.wait_ge(ring_free, after)
                settle()
                m = MX[:, grp % 2]
                part = [NM[:, :, :, n].rearrange("p t j -> p j t") for n in range(3)]
                own.inc(nc.gpsimd.tensor_scalar(nmr[:], m, -1.0, None, ALU.mult))
                for n in range(2):
                    own.wait(pool)
                    settle()
                    own.inc(nc.gpsimd.tensor_copy(part[n], nmr[:]))
                    own.wait(pool)
                    own.inc(nc.gpsimd.tensor_tensor(nmr[:], nmr[:], part[n], ALU.subtract))
                own.wait(pool)
                settle()
                nc.gpsimd.tensor_copy(part[2], nmr[:]).then_inc(nm_ready, 1)

            NM_INCS = 5

            pool.wait_ge(const_in, 16 * (N_CONST + 1))
            pool.wait_ge(const_ready, 1)
            add_bias(0)
            rope(0, own, PRO_ORD["qk", 3, 0] + 1)
            negated_maxima(0, own, PRO_ORD["sc", 0, 3, TT - 1] + 1)
            HEAD = own.n
            PER = ROPE_INCS + G * NM_INCS
            assert HEAD == ROPE_INCS + NM_INCS

            def batch(b, last):
                _, _, order, _ = schedule(last)
                own = Tally(pool_own, HEAD + b * PER)
                for g in range(G):
                    if last and g == G - 1:
                        break
                    if g == 2 and not last:
                        rope(b + 1, own, ring_base(b) + order["qk", 3, 1] + 1)
                    negated_maxima(g + 1, own, ring_base(b) + order["sc", g + 1, 3, TT - 1] + 1)
                    if g == 0 and not last:
                        add_bias(b + 1)
                assert last or own.n == PER

            if B > 1:
                with pool.Fori(0, B - 1) as b:
                    batch(b, False)
            batch(B - 1, True)

        @block.vector
        def _(dve):
            own = Tally(dve_own)
            for A in (QP, KP):
                own.inc(nc.vector.memset(A[:], 0.0))
            own.inc(nc.vector.memset(VA[:], 0.0))
            own.wait(dve)
            nc.vector.memset(KP[:, :, :, HD:HD + 3], 1.0)
            nc.vector.memset(VA[:, :, :, HD:HD + 1], 1.0)
            dve.wait_ge(const_in, 16 * (N_CONST + 1))
            nc.vector.tensor_copy(identb[:], ident[:])
            nc.vector.tensor_copy(cosb[:], cs_in[:, 0])
            own.inc(nc.vector.tensor_copy(sinb[:], cs_in[:, 1]))
            own.wait(dve)
            nc.vector.tensor_scalar(sinb[:, :, 0:HD // 2], sinb[:, :, 0:HD // 2], -1.0, None,
                                    ALU.mult).then_inc(const_ready, 1)

            def stat(b, i, own):
                own.inc(nc.vector.bn_stats(stats[:, i, :], X[:, b * TT + i, :]))
                own.wait(dve)
                nc.vector.memset(dve_scratch[:], 0.0)
                own.inc(nc.vector.bn_aggr(mv[:, i, :], stats[:, i, :]))

            def normalise(b, own):
                own.wait(dve)
                own.inc(rsqrt_steps(nc, dve, own, rstd[:], nt1[:], nt2[:], mv[:, :, 1]))
                own.wait(dve)
                for i in range(TT):
                    nc.vector.tensor_scalar(XN[:, i, :], X[:, b * TT + i, :], mv[:, i, 0:1], rstd[:, i:i + 1],
                                            ALU.subtract, ALU.mult).then_inc(xn_ready, 1)

            STAT_INCS = 2 * TT + RSQRT_INCS + 1
            OT_INCS = 1

            def consume(item, u, k, b, own):
                dve.wait_ge(ring_full, k + 1)
                R = ring[u % 2]
                kind = item[0]
                if kind == "xt":
                    out = nc.vector.tensor_copy(XNT[:, :, 512 * item[1]:512 * item[1] + 512], R[:])
                elif kind == "qk":
                    t = slice(2 * item[1], 2 * item[1] + 2)
                    nc.vector.tensor_tensor(
                        QP[:, t, :, 0:HD], R[:, :, 0:H].rearrange("p t (h c) -> p t h c", c=HD),
                        b_q[:].rearrange("p (h c) -> p h c", c=HD).unsqueeze(1).to_broadcast([P, 2, NH, HD]), ALU.add)
                    out = nc.vector.tensor_copy(KP[:, t, :, 0:HD],
                                                R[:, :, H:2 * H].rearrange("p t (h c) -> p t h c", c=HD))
                elif kind == "qkT":
                    n = G * b + item[1]
                    if not (isinstance(n, int) and n == 0):
                        dve.wait_ge(qm_in, 64 * n)
                    nc.vector.tensor_copy(KT[item[1] % G][:], R[:, 1, :].bitcast(BF16))
                    out = nc.vector.tensor_copy(QS[:], R[:, 0, :].bitcast(BF16))
                elif kind == "v":
                    for half in range(2):
                        t = slice(4 * item[1] + 2 * half, 4 * item[1] + 2 * half + 2)
                        out = nc.vector.tensor_tensor(
                            VA[:, t, :, 0:HD], R[:, half, :].rearrange("p (t h c) -> p t h c", t=2, c=HD),
                            b_v[:].rearrange("p (h c) -> p h c", c=HD).unsqueeze(1).to_broadcast([P, 2, NH, HD]),
                            ALU.add)
                elif kind == "sc":
                    _, grp, j, qt = item
                    out = nc.vector.reduce_max(MX[:, grp % 2, j, qt:qt + 1], R[:], AX.XY)
                elif kind == "nm":
                    n = G * b + item[1]
                    if not (isinstance(n, int) and n == 0):
                        dve.wait_ge(nm_in, 64 * n)
                    out = nc.vector.tensor_copy(NS[:], R[0:12, 0, :].bitcast(BF16))
                elif kind == "ot":
                    _, g, qh = item
                    o = R[:, 0, :].rearrange("p (t j c) -> p t j c", t=4, c=QUAD)
                    own.inc(nc.vector.reciprocal(RD[:, qh], o[:, :, :, HD]))
                    own.wait(dve)
                    out = nc.vector.tensor_tensor(
                        AO[:, 4 * qh:4 * qh + 4, 64 * g:64 * g + 64].rearrange("p t (j c) -> p t j c", c=HD),
                        o[:, :, :, 0:HD], RD[:, qh].unsqueeze(3).to_broadcast([P, 4, 4, HD]), ALU.mult)
                elif kind == "aot":
                    out = nc.vector.tensor_copy(AOT[:, :, 512 * item[1]:512 * item[1] + 512], R[:])
                elif kind == "proj":
                    x = X[:, bass.ds(b * TT + 4 * item[1], 4), :]
                    dve.wait_ge(bias_added, TT * (b + 1))
                    out = nc.vector.tensor_tensor(x, R[:].rearrange("p a (c n) -> p (a c) n", n=H), x, ALU.add)
                out.then_inc(ring_free, 1)

            dve.wait_ge(x_in, 16)
            for i in range(TT):
                stat(0, i, own)
            normalise(0, own)
            for u, item in enumerate(PRO):
                consume(item, u, u, 0, own)
            HEAD = own.n
            PER = STAT_INCS + 2 * G * OT_INCS

            def batch(b, last):
                slots, flush, order, _ = schedule(last)
                own = Tally(dve_own, HEAD + b * PER)
                for g in range(G):
                    for s, items in enumerate(slots[g]):
                        for item in items:
                            consume(item, NPRO + order[item], ring_base(b) + order[item], b, own)
                        if g == 0 and not last:
                            if s == 5:
                                dve.wait_ge(x_in, 16 * (b + 2))
                            if 6 <= s < 6 + TT:
                                stat(b + 1, s - 6, own)
                            if s == 6 + TT:
                                normalise(b + 1, own)
                for item in flush:
                    consume(item, NPRO + order[item], ring_base(b) + order[item], b, own)
                assert last or own.n == PER

            if B > 1:
                with dve.Fori(0, B - 1) as b:
                    batch(b, False)
            batch(B - 1, True)

        @block.scalar
        def _(act):
            act.wait_ge(const_in, 16 * (N_CONST + 1))
            nc.scalar.activation(credit[:, 0:1], ident[:, 0:1], ACT.Exp).then_inc(st_free, ST_BANKS)
            nc.scalar.activation(credit[:, 1:2], ident[:, 0:1], ACT.Exp).then_inc(ot_ready, 1)

            def evacuate(b, half):
                act.wait_ge(pv_done, G * STEPS * b + TT * (half + 1) + P_STEPS)
                nc.scalar.copy(OT[:], pv_bank[:]).then_inc(ot_ready, 1)

            def batch(b, last):
                _, _, order, _ = schedule(last)
                for g in range(G):
                    for s in range(STEPS):
                        step = g * STEPS + s
                        for j in range(4):
                            n = 4 * step + j
                            if j == 0:
                                act.wait_ge(pv_done, G * STEPS * b + step + 1)
                            act.wait_ge(st_full, 4 * G * STEPS * b + n + 1)
                            nc.scalar.activation(PR[step % P_STEPS][:, j, :], st_bank[n % ST_BANKS][:], ACT.Exp,
                                                 scale=0.25).then_inc(st_free, 1)
                            if j == 0 and s % TT == 1 and step > 1:
                                half = step // TT - 1
                                if half == 0:
                                    act.wait_ge(ring_full, ring_base(b))
                                else:
                                    act.wait_ge(ring_full, ring_base(b) + order["ot", (half - 1) // 2, (half - 1) % 2] + 1)
                                evacuate(b, half)
                act.wait_ge(ring_full, ring_base(b) + order["ot", G - 1, 0] + 1)
                evacuate(b, 2 * G - 1)

            if B > 1:
                with act.Fori(0, B - 1) as b:
                    batch(b, False)
            batch(B - 1, True)

        @block.tensor
        def _(pe):
            pe.wait_ge(const_in, 16 * (N_CONST + 1))
            pe.wait_ge(const_ready, 1)

            def fill(item, u, k, b, order, at):
                if not (isinstance(k, int) and k < 2):
                    pe.wait_ge(ring_free, k - 1)
                R = ring[u % 2]
                kind = item[0]
                if kind == "xt":
                    if item[1] == 0:
                        pe.wait_ge(xn_ready, TT * (b + item[2] + 1))
                    for h in range(KH):
                        for t in range(4):
                            out = nc.tensor.transpose(R[:, h, P * t:P * t + P],
                                                      XN[:, 4 * item[1] + t, P * h:P * h + P], ident[:])
                elif kind == "qk":
                    if item[1] == 0:
                        pe.wait_ge(ring_free, at + order["xt", 1, item[2]] + 1)
                    for t in range(2):
                        i = 2 * item[1] + t
                        for h in range(KH):
                            out = nc.tensor.matmul(R[:, t, :], XNT[:, h, P * i:P * i + P], w_qk[:, h, :],
                                                   start=(h == 0), stop=(h == KH - 1))
                elif kind == "v":
                    for t in range(4):
                        i = 4 * item[1] + t
                        for h in range(KH):
                            out = nc.tensor.matmul(R[:, t // 2, H * (t % 2):H * (t % 2) + H],
                                                   XNT[:, h, P * i:P * i + P], w_v[:, h, :],
                                                   start=(h == 0), stop=(h == KH - 1))
                elif kind == "qkT":
                    g = item[1] % G
                    pe.wait_ge(rope_done, 2 * (b + item[1] // G + 1))
                    for n, A in enumerate((QP, KP)):
                        for t in range(TT):
                            out = nc.tensor.transpose(
                                R[:, n, :].bitcast(BF16)[:, P * t:P * t + P],
                                A[:, t, 4 * g:4 * g + 4, :].rearrange("p h c -> p (h c)"), identb[:])
                elif kind == "sc":
                    _, grp, j, qt = item
                    if j == 0 and qt == 0:
                        pe.wait_ge(qm_in, 64 * (G * b + grp + 1))
                    for n in range(2):
                        out = nc.tensor.matmul(R[:, n, :], QM[grp % G][j][:, P * qt:P * qt + P],
                                               KT[grp % G][:, 512 * n:512 * n + 512], start=True, stop=True)
                elif kind == "nm":
                    pe.wait_ge(nm_ready, G * b + item[1] + 1)
                    for t in range(TT):
                        out = nc.tensor.transpose(R[0:12, 0, :].bitcast(BF16)[:, P * t:P * t + P],
                                                  NM[:, t].rearrange("p j n -> p (j n)"), identb[:])
                elif kind == "ot":
                    _, g, qh = item
                    pe.wait_ge(ot_ready, 2 * G * b + 2 * g + qh + 2)
                    for t in range(4):
                        out = nc.tensor.transpose(R[:, 0, P * t:P * t + P], OT[:, P * t:P * t + P], ident[:])
                elif kind == "aot":
                    pe.wait_ge(ring_free, at + order["ot", G - 1, 1] + 1)
                    for h in range(KH):
                        for t in range(4):
                            out = nc.tensor.transpose(R[:, h, P * t:P * t + P],
                                                      AO[:, 4 * item[1] + t, P * h:P * h + P], ident[:])
                elif kind == "proj":
                    pe.wait_ge(ring_free, at + order["aot", item[1]] + 1)
                    for t in range(4):
                        i = 4 * item[1] + t
                        for h in range(KH):
                            out = nc.tensor.matmul(R[:, t // 2, H * (t % 2):H * (t % 2) + H],
                                                   AOT[:, h, P * i:P * i + P], w_o[:, h, :],
                                                   start=(h == 0), stop=(h == KH - 1))
                out.then_inc(ring_full, 1)

            for u, item in enumerate(PRO):
                fill(item, u, u, 0, PRO_ORD, 0)
            nc.tensor.matmul(pv_bank[:, 0:P], identb[:], identb[:], start=True, stop=True).then_inc(pv_done, P_STEPS)

            def score_bank(b, g, s, j):
                n = 4 * (g * STEPS + s) + j
                back = {0: 0, 1: -2, 2: -1}.get(n, n - 2)
                pe.wait_ge(st_free, 4 * G * STEPS * b + ST_BANKS + back)
                qh, kt = s // TT, s % TT
                nc.tensor.matmul(st_bank[n % ST_BANKS][:], KT[g][:, P * kt:P * kt + P],
                                 QM[g][j][:, 512 * qh:512 * qh + 512], start=True, stop=True).then_inc(st_full, 1)

            def weigh_values(b, g, s):
                step = g * STEPS + s
                kt = s % TT
                if kt == 0:
                    pe.wait_ge(ot_ready, 2 * G * b + step // TT + 1)
                    if step == 0:
                        pe.wait_ge(ring_free, ring_base(b))
                pe.wait_ge(st_free, 4 * G * STEPS * b + 4 * (step + 1) + ST_BANKS)
                for j in range(4):
                    out = nc.tensor.matmul(pv_bank[QUAD * j:QUAD * j + QUAD, :], VA[:, kt, 4 * g + j, :],
                                           PR[step % P_STEPS][:, j, :], start=(kt == 0), stop=(kt == TT - 1))
                return out

            def batch(b, last):
                slots, flush, order, _ = schedule(last)
                at = ring_base(b)

                def ring_item(item):
                    fill(item, NPRO + order[item], at + order[item], b, order, at)
                for g in range(G):
                    pe.wait_ge(nm_in, 64 * (G * b + g + 1))
                    for s in range(STEPS):
                        items = slots[g][s]
                        cut = (len(items) + 1) // 2
                        score_bank(b, g, s, 0)
                        score_bank(b, g, s, 1)
                        for item in items[:cut]:
                            ring_item(item)
                        score_bank(b, g, s, 2)
                        score_bank(b, g, s, 3)
                        for item in items[cut:]:
                            ring_item(item)
                        before = g * STEPS + s - 1
                        if before >= 0:
                            finish_step(b, before)
                finish_step(b, G * STEPS - 1)
                for item in flush:
                    ring_item(item)

            def finish_step(b, step):
                weigh_values(b, step // STEPS, step % STEPS).then_inc(pv_done, 1)

            if B > 1:
                with pe.Fori(0, B - 1) as b:
                    batch(b, False)
            batch(B - 1, True)


D, F, E = 256, 512, 16
KD, KF = D // P, F // P
CAP = 128


def gates(nc, d, X, SC, B):
    T = 1024
    TT = T // P
    CT = 4
    NC = TT // CT
    ctx = ExitStack()
    with ctx:
        def sb(name, shape, dt):
            return ctx.enter_context(nc.sbuf_tensor("gate_" + name, shape, dt))

        def sem(name):
            return ctx.enter_context(nc.semaphore("gate_" + name))

        ident = sb("ident", [P, P], F32)
        gw = sb("gw", [P, KD, E], F32)
        stats = sb("stats", [P, TT, 6], F32)
        mv = sb("mv", [P, TT, 2], F32)
        rstd = sb("rstd", [P, TT], F32)
        nt1 = sb("nt1", [P, TT], F32)
        nt2 = sb("nt2", [P, TT], F32)
        XN = [sb(f"XN{i}", [P, CT, D], F32) for i in range(NC)]
        XT = [sb(f"XT{i}", [P, KD, CT * P], F32) for i in range(NC)]
        shifted = [sb(f"shifted{i}", [P, CT, E], F32) for i in range(NC)]
        powers = [sb(f"powers{i}", [P, CT, E], F32) for i in range(NC)]
        top = sb("top", [P, CT], F32)
        dve_scratch = sb("dve_scratch", [P, 1], F32)
        total = sb("total", [P, CT], F32)
        turned = [ctx.enter_context(nc.psum_tensor(f"turned{i}", [P, KD, 512], F32)) for i in range(NC)]
        logit = [ctx.enter_context(nc.psum_tensor(f"logit{i}", [P, 512], F32)) for i in range(NC)]

        const_in = sem("const_in")
        xn_ready = sem("xn_ready")
        xn_out = [sem(f"xn_out{i}") for i in range(NC)]
        turned_full = sem("turned_full")
        xt_ready = sem("xt_ready")
        logit_full = sem("logit_full")
        shifted_ready = sem("shifted_ready")
        powers_ready = sem("powers_ready")
        norm_own = sem("norm_own")
        softmax_own = sem("softmax_own")

        block = ctx.enter_context(nc.Block())

        def chunks(engine, body):
            for h in range(NC):
                body(0, h, h)
            if B > 1:
                with engine.Fori(1, B) as b:
                    for h in range(NC):
                        body(b, h, NC * b + h)

        def later(n, back):
            return not isinstance(n, int) or n >= back

        @block.sync
        def _(sp):
            sp.dma_start(ident[:], d["ident"]).then_inc(const_in, 16)
            sp.dma_start(gw[:], d["gwT"].rearrange("(k p) e -> p k e", p=P)).then_inc(const_in, 16)

            def store(b, h, n):
                sp.wait_ge(xn_ready, CT * (n + 1))
                sp.dma_start(d["xn2"][bass.ds(n * CT * P, CT * P), :].rearrange("(i p) h -> p i h", p=P),
                             XN[h][:]).then_inc(xn_out[h], 16)
            chunks(sp, store)
            for h in range(NC):
                sp.wait_ge(xn_out[h], 16 * B)

        @block.vector
        def _(dve):
            def normalise(b):
                own = Tally(norm_own, b * (TT + 2 + RSQRT_INCS))
                for i in range(TT):
                    own.inc(nc.vector.bn_stats(stats[:, i, :],
                                               X[:, bass.ds(b * TT + i, 1), :].rearrange("p a h -> p (a h)")))
                own.wait(dve)
                nc.vector.memset(dve_scratch[:], 0.0)
                for i in range(TT):
                    last = nc.vector.bn_aggr(mv[:, i, :], stats[:, i, :])
                own.inc(last)
                own.wait(dve)
                own.inc(rsqrt_steps(nc, dve, own, rstd[:], nt1[:], nt2[:], mv[:, :, 1]))
                own.wait(dve)
                for h in range(NC):
                    if not (isinstance(b, int) and b == 0):
                        dve.wait_ge(xn_out[h], 16 * b)
                        dve.wait_ge(turned_full, NC * (b - 1) + h + 1)
                    for t in range(CT):
                        i = CT * h + t
                        nc.vector.tensor_scalar(XN[h][:, t, :], X[:, bass.ds(b * TT + i, 1), :].rearrange("p a h -> p (a h)"),
                                                mv[:, i, 0:1], rstd[:, i:i + 1],
                                                ALU.subtract, ALU.mult).then_inc(xn_ready, 1)
                assert own.n == TT + 2 + RSQRT_INCS

            def softmax(b, h, n):
                own = Tally(softmax_own, n * 4)
                dve.wait_ge(logit_full, n + 1)
                logits = logit[h][:, 0:CT * E].rearrange("p (t e) -> p t e", e=E)
                own.inc(nc.vector.reduce_max(top[:], logits, AX.X))
                own.wait(dve)
                nc.vector.tensor_tensor(shifted[h][:], logits, top[:].unsqueeze(2).to_broadcast([P, CT, E]),
                                        ALU.subtract).then_inc(shifted_ready, 1)
                dve.wait_ge(powers_ready, n + 1)
                own.inc(nc.vector.reduce_sum(total[:], powers[h][:], AX.X))
                own.wait(dve)
                own.inc(nc.vector.reciprocal(total[:], total[:]))
                own.wait(dve)
                own.inc(nc.vector.tensor_tensor(SC[:, CT * h:CT * h + CT, bass.ds(b * E, E)], powers[h][:],
                                                total[:].unsqueeze(2).to_broadcast([P, CT, E]), ALU.mult))
                own.wait(dve)

            normalise(0)
            if B > 1:
                with dve.Fori(0, B - 1) as b:
                    normalise(b + 1)
                    for h in range(NC):
                        softmax(b, h, NC * b + h)
            for h in range(NC):
                softmax(B - 1, h, NC * (B - 1) + h)

        @block.scalar
        def _(act):
            def move(b, h, n):
                act.wait_ge(turned_full, n + 1)
                if later(n, NC):
                    act.wait_ge(logit_full, n - 1)
                nc.scalar.copy(XT[h][:], turned[h][:]).then_inc(xt_ready, 1)
                act.wait_ge(shifted_ready, n + 1)
                nc.scalar.activation(powers[h][:], shifted[h][:], ACT.Exp).then_inc(powers_ready, 1)
            chunks(act, move)

        @block.tensor
        def _(pe):
            pe.wait_ge(const_in, 32)

            def logits(b, h, n):
                pe.wait_ge(xn_ready, CT * (n + 1))
                if later(n, NC):
                    pe.wait_ge(xt_ready, n - 1)
                for k in range(KD):
                    for t in range(CT):
                        out = nc.tensor.transpose(turned[h][:, k, P * t:P * t + P], XN[h][:, t, P * k:P * k + P], ident[:])
                out.then_inc(turned_full, 1)
                pe.wait_ge(xt_ready, n + 1)
                if later(n, NC):
                    pe.wait_ge(shifted_ready, n - 1)
                for t in range(CT):
                    for k in range(KD):
                        out = nc.tensor.matmul(logit[h][:, E * t:E * t + E], XT[h][:, k, P * t:P * t + P], gw[:, k, :],
                                               start=(k == 0), stop=(k == KD - 1))
                out.then_inc(logit_full, 1)
            chunks(pe, logits)


def feed_forward(nc, d, X, SC, WT, IX, B, shared):
    T = 1024
    TT = T // P
    BE = B * E
    CT = 4 if shared else B // 2
    N = CT * P
    HALVES = 2
    K = HALVES if shared else 2 * HALVES
    R = B if shared else E // 2
    FR = mybir.dt.float32r
    ROUNDS = CAP // 8
    tag = "sh_" if shared else "ex_"
    ctx = ExitStack()
    with ctx:
        def sb(name, shape, dt):
            return ctx.enter_context(nc.sbuf_tensor(tag + name, shape, dt))

        def sem(name):
            return ctx.enter_context(nc.semaphore(tag + name))

        ident = sb("ident", [P, P], F32)
        W = [sb("Wg", [P, KD, F], F32), sb("Wu", [P, KD, F], F32), sb("Wd", [P, KF, D], F32)]
        SETS = 1 if shared else 2
        WH = [[sb(f"WH{q}{i}", list(w.shape), FR) for i, w in enumerate(W)] for q in range(SETS)]
        WL = [[sb(f"WL{q}{i}", list(w.shape), FR) for i, w in enumerate(W)] for q in range(SETS)]
        XG = [sb(f"XG{c}", [P, CT, D], F32) for c in range(2)]
        XH = [sb(f"XH{c}", [P, KD, N], FR) for c in range(2)]
        XL = [sb(f"XL{c}", [P, KD, N], FR) for c in range(2)]
        GL = [sb(f"GL{c}", [P, N], F32) for c in range(2)]
        HF = [sb(f"HF{c}", [P, N], F32) for c in range(2)]
        HH = [sb(f"HH{c}", [P, KF, N], FR) for c in range(2)]
        HL = [sb(f"HL{c}", [P, KF, N], FR) for c in range(2)]
        YS = [sb(f"YS{c}", [P, CT, D], F32) for c in range(2)]
        if shared:
            sct = sb("sct", [BE, T], F32)
            vals = sb("vals", [BE, CAP], F32)
            inds = sb("inds", [BE, CAP], U32)
            indf = sb("indf", [BE, CAP], F32)
            row0 = sb("row0", [BE, 1], F32)
            v8 = sb("v8", [BE, 8], F32)
            i8 = sb("i8", [BE, 8], U32)
        else:
            rows_in = sb("rows_in", [P, B], U32)
            rows_out = sb("rows_out", [P, B], U32)
            WC = [sb(f"WC{q}", [P, B], F32) for q in range(2)]
            pool_scratch = sb("pool_scratch", [P, 1], F32)

        gu = [ctx.enter_context(nc.psum_tensor(f"{tag}gu{i}", [P, 2, 512], F32)) for i in range(2)]
        turned = ctx.enter_context(nc.psum_tensor(f"{tag}turned", [P, KD, 512], F32))
        y = ctx.enter_context(nc.psum_tensor(f"{tag}y", [P, 2, 512], F32))

        const_in = sem("const_in")
        w_in = sem("w_in")
        wh_ready = sem("wh_ready")
        wl_ready = sem("wl_ready")
        x_in = [sem(f"x_in{c}") for c in range(2)]
        turned_full = sem("turned_full")
        xh_ready = sem("xh_ready")
        xl_ready = sem("xl_ready")
        gu_full = sem("gu_full")
        gelu_ready = sem("gelu_ready")
        hf_ready = sem("hf_ready")
        hh_ready = sem("hh_ready")
        hl_ready = sem("hl_ready")
        y_full = sem("y_full")
        ys_ready = sem("ys_ready")
        y_out = [sem(f"y_out{c}") for c in range(2)]
        ic_ready = sem("ic_ready")
        oc_ready = sem("oc_ready")
        wc_ready = sem("wc_ready")
        settled = sem("settled")
        sct_full = sem("sct_full")
        sct_ready = sem("sct_ready")
        sel_ready = sem("sel_ready")
        sel_full = sem("sel_full")
        sel_done = sem("sel_done")
        own_sem = sem("own")

        block = ctx.enter_context(nc.Block())

        def groups(engine, body):
            body(0, True, R == 1)
            if R > 2:
                with engine.Fori(1, R - 1) as r:
                    body(r, False, False)
            if R > 1:
                body(R - 1, False, True)

        Y_INC = CT if not shared else 1
        X_INC = 16 if shared else 16 * CT

        def slot_of(k):
            return k % 2

        def expert(r, k):
            return 2 * r + k // HALVES

        def load_weights(sp, e):
            if shared:
                src = [d["SgT"], d["SuT"], d["SdT"]]
            else:
                src = [d["WgT"][bass.ds(e * D, D), :], d["WuT"][bass.ds(e * D, D), :], d["WdT"][bass.ds(e * F, F), :]]
            for w, s in zip(W, src):
                sp.dma_start(w[:], s.rearrange("(k p) n -> p k n", p=P)).then_inc(w_in, 16)

        @block.sync
        def _(sp):
            sp.dma_start(ident[:], d["ident"]).then_inc(const_in, 16)
            if shared:
                sp.dma_start(row0[:], d["row0"][0:BE, :]).then_inc(const_in, 16)
                load_weights(sp, 0)

                def load(r, k):
                    n = r * K + k
                    if not (isinstance(n, int) and n < 2):
                        sp.wait_ge(turned_full, n - 1)
                    sp.dma_start(XG[slot_of(k)][:], d["xn2"][bass.ds(n * N, N), :].rearrange("(i p) h -> p i h", p=P)
                                 ).then_inc(x_in[slot_of(k)], 16)

                def store(r, k):
                    n = r * K + k
                    sp.wait_ge(ys_ready, n + 1)
                    sp.dma_start(d["out"][bass.ds(n * N, N), :].rearrange("(i p) h -> p i h", p=P),
                                 YS[slot_of(k)][:]).then_inc(y_out[slot_of(k)], 16)
                load(0, 0)
                load(0, 1)

                def group(r, first, last):
                    for k in range(K):
                        if not (last and k >= K - 2):
                            load(r if k < K - 2 else r + 1, (k + 2) % K)
                        if not (first and k == 0):
                            store(r if k else r - 1, (k - 1) % K)
                groups(sp, group)
                store(R - 1, K - 1)
                for c in range(2):
                    sp.wait_ge(y_out[c], 16 * R * K // 2)
            else:
                load_weights(sp, 0)

                def load_next(e):
                    sp.wait_ge(wl_ready, 3 * (e + 1))
                    load_weights(sp, e + 1)
                load_next(0)
                if E > 2:
                    with sp.Fori(1, E - 1) as e:
                        load_next(e)

        @block.gpsimd
        def _(pool):
            if shared:
                return

            pool.wait_ge(const_in, 16)

            def settle(own):
                if not isinstance(own.base, int) or own.base + own.n > 0:
                    own.wait(pool)
                own.inc(nc.gpsimd.tensor_tensor(pool_scratch[:], ident[:, 0:1], ident[:, 0:1], ALU.mult))

            def take_rows(IC, e, own, taken):
                settle(own)
                nc.gpsimd.tensor_copy(IC[:], IX[:, :, bass.ds(e, 1)].rearrange("p b a -> p (b a)")
                                      ).then_inc(taken, 1)
                pool.wait_ge(taken, e + 1)

            def gather(r, k, own):
                n = r * K + k
                if k % HALVES == 0:
                    if not (isinstance(n, int) and n == 0):
                        for c in range(2):
                            pool.wait_ge(x_in[c], X_INC * expert(r, k))
                    take_rows(rows_in, expert(r, k), own, ic_ready)
                if not (isinstance(n, int) and n < 2):
                    pool.wait_ge(turned_full, n - 1)
                settle(own)
                for t in range(CT):
                    b = CT * (k % HALVES) + t
                    nc.gpsimd.indirect_dma_start(
                        out=XG[k % 2][:, t, :], out_offset=None, in_=d["xn2"],
                        in_offset=bass.IndirectOffsetOnAxis(ap=rows_in[:, b:b + 1], axis=0)).then_inc(x_in[k % 2], 16)

            def scatter(r, k, own):
                n = r * K + k
                e = expert(r, k)
                if k % HALVES == 0:
                    if not (isinstance(n, int) and n == 0):
                        for c in range(2):
                            pool.wait_ge(y_out[c], 16 * CT * e)
                    take_rows(rows_out, e, own, oc_ready)
                pool.wait_ge(ys_ready, Y_INC * (n + 1))
                if not (isinstance(e, int) and e == 0):
                    pool.wait_ge(y_out[k % 2], 16 * CT * e)
                settle(own)
                for t in range(CT):
                    b = CT * (k % HALVES) + t
                    nc.gpsimd.indirect_dma_start(
                        out=d["out"], out_offset=bass.IndirectOffsetOnAxis(ap=rows_out[:, b:b + 1], axis=0),
                        in_=YS[k % 2][:, t, :], in_offset=None, compute_op=ALU.add).then_inc(y_out[k % 2], 16)
            own = Tally(settled)
            gather(0, 0, own)
            gather(0, 1, own)
            HEAD = own.n
            PER = 2 * K + 2 * (K // HALVES)

            def group(r, first, last):
                own = Tally(settled, HEAD if first else HEAD + r * PER - 1)
                for k in range(K):
                    if not (last and k >= K - 2):
                        gather(r if k < K - 2 else r + 1, (k + 2) % K, own)
                    if not (first and k == 0):
                        scatter(r if k else r - 1, (k - 1) % K, own)
            groups(pool, group)
            own = Tally(settled, HEAD + R * PER - 1 - 3)
            scatter(R - 1, K - 1, own)
            for c in range(2):
                pool.wait_ge(y_out[c], 16 * CT * R * K // 2)

        @block.scalar
        def _(act):
            def split_weights(e, q, i):
                act.wait_ge(w_in, 48 * (e + 1))
                nc.scalar.copy(WH[q][i][:], W[i][:]).then_inc(wh_ready, 1)

            def split_tokens(r, k):
                n = r * K + k
                act.wait_ge(turned_full, n + 1)
                nc.scalar.copy(XH[k % 2][:], turned[:, :, 0:N]).then_inc(xh_ready, 1)

            def gelu(n, f):
                act.wait_ge(gu_full, KF * n + f + 1)
                nc.scalar.activation(GL[f % 2][:], gu[f % 2][:, 0, 0:N], ACT.Gelu).then_inc(gelu_ready, 1)

            def high(n, k, f):
                act.wait_ge(hf_ready, KF * n + f + 1)
                nc.scalar.copy(HH[k % 2][:, f, :], HF[f % 2][:]).then_inc(hh_ready, 1)

            for i in range(3):
                split_weights(0, 0, i)
            split_tokens(0, 0)

            def group(r, first, last):
                for k in range(K):
                    n = r * K + k
                    final = last and k == K - 1
                    more = not shared and not (last and k >= K - HALVES)
                    e, q = expert(r, k) + 1, (k // HALVES + 1) % 2
                    gelu(n, 0)
                    gelu(n, 1)
                    high(n, k, 0)
                    if not final:
                        split_tokens(r if k < K - 1 else r + 1, (k + 1) % K)
                    gelu(n, 2)
                    high(n, k, 1)
                    gelu(n, 3)
                    high(n, k, 2)
                    if more and k % HALVES == 0:
                        if not (isinstance(n, int) and n == 0):
                            act.wait_ge(y_full, n)
                        split_weights(e, q, 0)
                    if more and k % HALVES == 1:
                        split_weights(e, q, 2)
                    high(n, k, 3)
                    if more and k % HALVES == 0:
                        split_weights(e, q, 1)
            groups(act, group)

        @block.vector
        def _(dve):
            def split_weights(e, q, i):
                dve.wait_ge(wh_ready, 3 * e + i + 1)
                nc.vector.tensor_tensor(WL[q][i][:], W[i][:], WH[q][i][:].bitcast(F32),
                                        ALU.subtract).then_inc(wl_ready, 1)
                if not shared and i == 2:
                    if not (isinstance(e, int) and e < 2):
                        dve.wait_ge(ys_ready, Y_INC * HALVES * (e - 1))
                    nc.vector.tensor_copy(WC[q][:], WT[:, :, bass.ds(e, 1)].rearrange("p b a -> p (b a)")
                                          ).then_inc(wc_ready, 1)

            def split_tokens(r, k):
                n = r * K + k
                dve.wait_ge(xh_ready, n + 1)
                nc.vector.tensor_tensor(XL[k % 2][:], turned[:, :, 0:N], XH[k % 2][:].bitcast(F32),
                                        ALU.subtract).then_inc(xl_ready, 1)

            def product(n, f):
                i = KF * n + f
                if not (isinstance(i, int) and i < 2):
                    dve.wait_ge(hl_ready, i - 1)
                dve.wait_ge(gelu_ready, i + 1)
                nc.vector.tensor_tensor(HF[f % 2][:], GL[f % 2][:], gu[f % 2][:, 1, 0:N], ALU.mult).then_inc(hf_ready, 1)

            def low(n, k, f):
                dve.wait_ge(hh_ready, KF * n + f + 1)
                nc.vector.tensor_tensor(HL[k % 2][:, f, :], HF[f % 2][:], HH[k % 2][:, f, :].bitcast(F32),
                                        ALU.subtract).then_inc(hl_ready, 1)

            def result(r, k):
                n = r * K + k
                dve.wait_ge(y_full, n + 1)
                if not (isinstance(n, int) and n < 2):
                    dve.wait_ge(y_out[k % 2], X_INC * (r * (K // 2) + k // 2))
                yv = y[:].rearrange("p a (c n) -> p (a c) n", n=D)
                if shared:
                    nc.vector.tensor_tensor(YS[k % 2][:], yv, X[:, bass.ds(n * CT, CT), :], ALU.add).then_inc(ys_ready, 1)
                else:
                    dve.wait_ge(wc_ready, expert(r, k) + 1)
                    for t in range(CT):
                        b = CT * (k % HALVES) + t
                        nc.vector.tensor_scalar(YS[k % 2][:, t, :], yv[:, t, :], WC[(k // HALVES) % 2][:, b:b + 1],
                                                None, ALU.mult).then_inc(ys_ready, 1)

            CHUNKS = R * K
            TURNS = -(-ROUNDS // CHUNKS)

            def select(s, own):
                own.inc(nc.vector.max(v8[:], sct[:]))
                own.wait(dve)
                nc.vector.tensor_copy(vals[:, bass.ds(8 * s, 8)], v8[:])
                own.inc(nc.vector.max_index(i8[:], v8[:], sct[:]))
                own.wait(dve)
                nc.vector.tensor_copy(inds[:, bass.ds(8 * s, 8)], i8[:])
                own.inc(nc.vector.match_replace(sct[:], v8[:], sct[:], -1.0))
                own.wait(dve)

            if shared:
                dve.wait_ge(sct_full, 1)
                nc.vector.tensor_copy(sct[:], y[0:BE].rearrange("p a n -> p (a n)")).then_inc(sct_ready, 1)
                dve.wait_ge(sct_ready, 1)
            for i in range(3):
                split_weights(0, 0, i)
            split_tokens(0, 0)

            def group(r, first, last):
                own = Tally(own_sem, 3 * TURNS * K * r)
                for k in range(K):
                    n = r * K + k
                    final = last and k == K - 1
                    more = not shared and not (last and k >= K - HALVES)
                    e, q = expert(r, k) + 1, (k // HALVES + 1) % 2
                    product(n, 0)
                    product(n, 1)
                    low(n, k, 0)
                    if not final:
                        split_tokens(r if k < K - 1 else r + 1, (k + 1) % K)
                    product(n, 2)
                    low(n, k, 1)
                    if not (first and k == 0):
                        result(r if k else r - 1, (k - 1) % K)
                    product(n, 3)
                    low(n, k, 2)
                    if more:
                        split_weights(e, q, 0 if k % HALVES == 0 else 2)
                    low(n, k, 3)
                    if more and k % HALVES == 0:
                        split_weights(e, q, 1)
                    if shared:
                        for s in range(TURNS):
                            select(TURNS * n + s, own)
            groups(dve, group)
            result(R - 1, K - 1)
            if shared:
                assert TURNS * CHUNKS == ROUNDS
                own = Tally(own_sem, 3 * ROUNDS)
                own.inc(nc.vector.tensor_copy(indf[:], inds[:]))
                own.wait(dve)
                dve.wait_ge(const_in, 32)
                nc.vector.tensor_scalar(indf[:], indf[:], row0[:], None, ALU.add).then_inc(sel_ready, 1)
                dve.wait_ge(sel_full, 1)
                nc.vector.tensor_copy(WT[:].rearrange("p b e -> p (b e)"), turned[:, 0, 0:BE])
                nc.vector.tensor_copy(IX[:].rearrange("p b e -> p (b e)"), turned[:, 1, 0:BE])

        @block.tensor
        def _(pe):
            pe.wait_ge(const_in, 32 if shared else 16)
            if shared:
                for t in range(TT):
                    out = nc.tensor.transpose(y[0:BE, t // 4, P * (t % 4):P * (t % 4) + P], SC[:, t, :], ident[:])
                out.then_inc(sct_full, 1)

            def turn_tokens(r, k):
                n = r * K + k
                pe.wait_ge(x_in[k % 2], X_INC * (r * (K // 2) + k // 2 + 1))
                if not (isinstance(n, int) and n == 0):
                    pe.wait_ge(xl_ready, n)
                for c in range(KD):
                    for t in range(CT):
                        out = nc.tensor.transpose(turned[:, c, P * t:P * t + P], XG[k % 2][:, t, P * c:P * c + P], ident[:])
                out.then_inc(turned_full, 1)

            def three(out, hi, lo, stationary, moving, first, last):
                a_hi, a_lo = hi[0][stationary], lo[0][stationary]
                b_hi, b_lo = hi[1][moving], lo[1][moving]
                nc.tensor.matmul(out, a_hi, b_hi, start=first, stop=False)
                nc.tensor.matmul(out, a_hi, b_lo, start=False, stop=False)
                return nc.tensor.matmul(out, a_lo, b_hi, start=False, stop=last)

            def up(n, k, q, f):
                i = KF * n + f
                if not (isinstance(i, int) and i < 2):
                    pe.wait_ge(hf_ready, i - 1)
                for m in range(2):
                    for c in range(KD):
                        out = three(gu[f % 2][:, m, 0:N], (WH[q][m], XH[k % 2]), (WL[q][m], XL[k % 2]),
                                    (slice(None), c, slice(P * f, P * f + P)), (slice(None), c, slice(None)),
                                    c == 0, c == KD - 1)
                out.then_inc(gu_full, 1)

            def down(r, k):
                n = r * K + k
                q = (k // HALVES) % 2 if not shared else 0
                pe.wait_ge(hl_ready, KF * (n + 1))
                if not shared or (isinstance(n, int) and n == 0):
                    pe.wait_ge(wl_ready, 3 * ((expert(r, k) if not shared else 0) + 1))
                if not (isinstance(n, int) and n == 0):
                    pe.wait_ge(ys_ready, Y_INC * n)
                if shared and isinstance(n, int) and n == 0:
                    pe.wait_ge(sct_ready, 1)
                for t in range(CT):
                    for f in range(KF):
                        out = three(y[:, t // 2, D * (t % 2):D * (t % 2) + D], (HH[k % 2], WH[q][2]), (HL[k % 2], WL[q][2]),
                                    (slice(None), f, slice(P * t, P * t + P)), (slice(None), f, slice(None)),
                                    f == 0, f == KF - 1)
                out.then_inc(y_full, 1)

            turn_tokens(0, 0)

            def group(r, first, last):
                for k in range(K):
                    n = r * K + k
                    q = (k // HALVES) % 2 if not shared else 0
                    if k % HALVES == 0 and (first or not shared):
                        pe.wait_ge(wl_ready, 3 * (expert(r, k) if not shared else 0) + 2)
                    pe.wait_ge(xl_ready, n + 1)
                    up(n, k, q, 0)
                    up(n, k, q, 1)
                    if not (last and k == K - 1):
                        turn_tokens(r if k < K - 1 else r + 1, (k + 1) % K)
                    if not (first and k == 0):
                        down(r if k else r - 1, (k - 1) % K)
                    up(n, k, q, 2)
                    up(n, k, q, 3)
            groups(pe, group)
            down(R - 1, K - 1)
            if shared:
                pe.wait_ge(sel_ready, 1)
                nc.tensor.transpose(turned[:, 0, 0:BE], vals[:], ident[0:BE, 0:BE])
                nc.tensor.transpose(turned[:, 1, 0:BE], indf[:], ident[0:BE, 0:BE]).then_inc(sel_full, 1)


def program(nc, d, B):
    TT = 1024 // P
    with ExitStack() as ctx:
        WT = ctx.enter_context(nc.sbuf_tensor("taken_scores", [P, B, E], F32))
        IX = ctx.enter_context(nc.sbuf_tensor("taken_rows", [P, B, E], U32))
        with ExitStack() as early:
            X = early.enter_context(nc.sbuf_tensor("X", [P, B * TT, D], F32))
            attention(nc, d, X, B)
            SC = early.enter_context(nc.sbuf_tensor("gate_scores", [P, TT, B * E], F32))
            gates(nc, d, X, SC, B)
            feed_forward(nc, d, X, SC, WT, IX, B, True)
        feed_forward(nc, d, None, None, WT, IX, B, False)


def kernel(**inputs):
    import numpy as np
    import concourse.bacc as bacc
    from concourse.bass_utils import run_bass_kernel_spmd

    a = {n.split("_", 2)[2]: np.asarray(v) for n, v in inputs.items()}
    B, T, H = a["hidden_states"].shape
    arrays = {
        "x": a["hidden_states"].reshape(B * T, H),
        **{n: a[n] for n in ("cos", "sin", "wq", "bq", "wk", "wv", "bv", "wo", "bo")},
        "gwT": a["gate_w"].T,
        "WgT": a["Wg"].transpose(0, 2, 1).reshape(E * D, F), "WuT": a["Wu"].transpose(0, 2, 1).reshape(E * D, F),
        "WdT": a["Wd"].transpose(0, 2, 1).reshape(E * F, D),
        "SgT": a["Ws_g"].T, "SuT": a["Ws_u"].T, "SdT": a["Ws_d"].T,
        "ident": np.eye(P, dtype=np.float32),
        "row0": np.repeat(np.arange(B), E)[:, None].astype(np.float32) * np.float32(T),
    }
    arrays = {n: np.ascontiguousarray(v) for n, v in arrays.items()}
    nc = bacc.Bacc("TRN2", target_bir_lowering=False, num_devices=1)
    d = {n: nc.dram_tensor(n, v.shape, mybir.dt.from_np(v.dtype), kind="ExternalInput").ap() for n, v in arrays.items()}
    d["xn2"] = nc.dram_tensor("xn2", (B * T, H), F32, kind="Internal").ap()
    d["out"] = nc.dram_tensor("out", (B * T, H), F32, kind="ExternalOutput").ap()
    program(nc, d, B)
    r = run_bass_kernel_spmd(nc, [arrays], core_ids=[0])
    return r.results[0]["out"].reshape(B, T, H)
```

```python
import concourse.bass as bass
from concourse import mybir
from contextlib import ExitStack

F32 = mybir.dt.float32
BF16 = mybir.dt.bfloat16
FR = mybir.dt.float32r
I32 = mybir.dt.int32
U32 = mybir.dt.uint32
ALU = mybir.AluOpType
ACT = mybir.ActivationFunctionType
AX = mybir.AxisListType

P = 128
QUAD = 32
EPS = 1e-5
NEWTON_STEPS = 3
RSQRT_MAGIC = float(0x5F3759DF)
D, F, E = 256, 512, 16


class Tally:

    def __init__(self, sem, base=0):
        self.sem, self.base, self.n = sem, base, 0

    def inc(self, instruction):
        instruction.then_inc(self.sem, 1)
        self.n += 1

    def wait(self, engine):
        engine.wait_ge(self.sem, self.base + self.n)


def rsqrt_step(nc, k, y, tmp, half, var):
    if k == 0:
        return nc.vector.tensor_scalar(tmp, var, EPS, None, ALU.add)
    if k == 1:
        nc.vector.tensor_scalar(half, tmp, -0.5, None, ALU.mult)
        return nc.vector.tensor_scalar(y.bitcast(I32), tmp.bitcast(I32), 1, None, ALU.logical_shift_right)
    if k == 2:
        return nc.vector.tensor_scalar(y.bitcast(I32), y.bitcast(I32), -1.0, RSQRT_MAGIC, ALU.mult, ALU.add)
    if k % 3 == 0:
        return nc.vector.tensor_tensor(tmp, y, y, ALU.mult)
    if k % 3 == 1:
        return nc.vector.tensor_tensor(tmp, tmp, half, ALU.mult)
    return nc.vector.scalar_tensor_tensor(y, tmp, 1.5, y, ALU.add, ALU.mult)


RSQRT_STEPS = 3 + 3 * NEWTON_STEPS


def three(nc, out, hi, lo, stationary, moving, first, last):
    a_hi, a_lo = hi[0][stationary], lo[0][stationary]
    b_hi, b_lo = hi[1][moving], lo[1][moving]
    nc.tensor.matmul(out, a_hi, b_hi, start=first, stop=False)
    nc.tensor.matmul(out, a_hi, b_lo, start=False, stop=False)
    return nc.tensor.matmul(out, a_lo, b_hi, start=False, stop=last)


def attention(nc, d, SC, B):
    H, NH, HD = 256, 16, 16
    T = 1024
    TT = T // P
    G = NH // 4
    KH = H // P
    NQ = T // 512
    STEPS = NQ * TT
    ROPE_TILES = 2
    SC_TILES = 4 * TT
    LEAD = 10
    ST_BANKS = 3
    P_STEPS = 2

    def scores(grp, a, z):
        return [("sc", grp, n // TT, n % TT) for n in range(a, z)]

    def slot_items(g, prev, more):
        t = g + 1
        base = scores(t, LEAD, SC_TILES) + scores(t + 1, 0, 4) + [("nm", t)] + scores(t + 1, 4, LEAD)
        steps = [[] for _ in range(STEPS)]
        for n, item in enumerate(base):
            steps[n * STEPS // len(base)].append(item)
        extra = {3: [("ot", g - 1, 1)], 11: [("ot", g, 0)]}
        if g == 0:
            extra |= {1: [("qkT", 2)], 4: [("aot", 0)], 5: [("aot", 1)], 10: [("proj", 0)], 12: [("proj", 1)]}
        if g == 1:
            extra |= {1: [("qkT", 3)], 2: [("xt", 0, 1)], 4: [("xt", 1, 1)],
                      7: [("qk", 0, 1)], 10: [("qk", 1, 1)], 13: [("qk", 2, 1)]}
        if g == 2:
            extra |= {0: [("qk", 3, 1)], 6: [("qkT", G)], 9: [("x2t", 0)], 13: [("x2t", 1)]}
        if g == 3:
            extra |= {1: [("qkT", G + 1)], 5: [("lg", 0)], 6: [("lg", 1)]}
        for s, items in extra.items():
            steps[s] = items + steps[s]

        def kept(i):
            if not more and (i[0] in ("xt", "qk") or (i[0] in ("sc", "nm", "qkT") and i[1] >= G)):
                return False
            return prev or not (i[0] in ("aot", "proj", "x2t", "lg") or i[:2] == ("ot", -1))
        return [[i for i in st if kept(i)] for st in steps]

    PRO = ([("xt", 0, 0), ("xt", 1, 0)] + [("qk", n, 0) for n in (3, 0, 1, 2)] + [("qkT", 0), ("qkT", 1), ("v", 0), ("v", 1)]
           + scores(0, 0, SC_TILES) + scores(1, 0, 4) + [("nm", 0)] + scores(1, 4, LEAD))
    TAIL = [("ot", -1, 1), ("aot", 0), ("aot", 1), ("proj", 0), ("proj", 1), ("x2t", 0), ("x2t", 1), ("lg", 0), ("lg", 1)]

    def split_late(item):
        return item[0] == "aot" or (item[0] == "xt" and item[2] == 1)

    def by_scalar(item):
        return split_late(item) or item[0] == "x2t"

    KINDS = {"all": lambda item: True, "vector": lambda item: not by_scalar(item), "scalar": by_scalar,
             "split": split_late}

    class Turn:

        def __init__(self, b, prev=False, more=False):
            self.kind = b if isinstance(b, str) else "turn"
            self.slots = [slot_items(g, prev, more) for g in range(G)] if self.kind == "turn" else []
            self.flush = [("v", 0), ("v", 1)] if more else []
            self.order = {"prologue": PRO, "tail": TAIL,
                          "turn": [i for sl in self.slots for st in sl for i in st] + self.flush}[self.kind]
            self.b, self.prev = b, prev

        def total(self, kind="all"):
            return len([i for i in self.order if KINDS[kind](i)])

        def before(self, kind="all"):
            if self.kind == "prologue":
                return 0
            n = Turn("prologue").total(kind)
            if self.kind == "tail":
                return n + Turn(0, False, True).total(kind) + (B - 2) * Turn(1, True, True).total(kind) + \
                    Turn(1, True, False).total(kind)
            if not self.prev:
                return n
            return n + Turn(0, False, True).total(kind) + (self.b - 1) * Turn(1, True, True).total(kind)

        def upto(self, item, kind="all"):
            return self.before(kind) + len([i for i in self.order[:self.order.index(item) + 1] if KINDS[kind](i)])

        def pair(self, item):
            first = self if self.kind != "turn" or not self.prev else Turn(1, True, True)
            return (first.before() + self.order.index(item)) % 2

        def vector_done(self, item):
            assert not by_scalar(item)
            return self.upto(item, "vector")

    assert Turn(1, True, True).total() % 2 == 0 and B > 1

    def turns(engine, body):
        body(0, False, True)
        if B > 2:
            with engine.Fori(1, B - 1) as b:
                body(b, True, True)
        body(B - 1, True, False)

    ctx = ExitStack()
    with ctx:
        def sb(name, shape, dt):
            return ctx.enter_context(nc.sbuf_tensor("sb_" + name, shape, dt))

        def sem(name):
            return ctx.enter_context(nc.semaphore(name))

        ident = sb("ident", [P, P], F32)
        identb = sb("identb", [P, P], BF16)
        WH = sb("WH", [P, KH, 4 * H], FR)
        WL = sb("WL", [P, KH, 4 * H], FR)
        gw = sb("gw", [P, KH, E], F32)
        b_q = sb("b_q", [P, H], F32)
        b_v = sb("b_v", [P, H], F32)
        b_o = sb("b_o", [P, H], F32)
        cs_in = sb("cs_in", [P, 2, ROPE_TILES, HD], F32)
        cosb = sb("cosb", [P, ROPE_TILES, HD], BF16)
        sinb = sb("sinb", [P, ROPE_TILES, HD], BF16)
        XA = sb("XA", [P, TT, H], F32)
        XR = sb("XR", [P, TT, H], F32)
        XN = sb("XN", [P, TT, H], F32)
        XN2 = sb("XN2", [P, TT, H], F32)
        XH = sb("XH", [P, KH, T], FR)
        XL = sb("XL", [P, KH, T], FR)
        XT = sb("XT", [P, KH, T], F32)
        AH = sb("AH", [P, KH, T], FR)
        AL = sb("AL", [P, KH, T], FR)
        QP = sb("QP", [P, TT, NH, QUAD], BF16)
        KP = sb("KP", [P, TT, NH, QUAD], BF16)
        QS = sb("QS", [P, T], BF16)
        KT = [sb(f"KT{g}", [P, T], BF16) for g in range(G)]
        QM = [[sb(f"QM{g}{j}", [P, T], BF16) for j in range(4)] for g in range(G)]
        VA = sb("VA", [P, TT, NH, QUAD], F32)
        PR = [sb(f"PR{n}", [P, 4, 512], F32) for n in range(P_STEPS)]
        OT = sb("OT", [P, 512], F32)
        AO = sb("AO", [P, TT, H], F32)
        W_raw = AO[:].rearrange("p a c -> p (a c)").rearrange("p (k n) -> p k n", k=KH)
        NS = sb("NS", [12, T], BF16)
        MX = sb("MX", [P, 2, 4, TT], F32)
        NM = sb("NM", [P, TT, 4, 3], BF16)
        nmr = sb("nmr", [P, 4, TT], F32)
        RD = sb("RD", [P, 2, 4, 4], F32)
        stats = sb("stats", [P, TT, 6], F32)
        mv = sb("mv", [P, TT, 2], F32)
        rstd = sb("rstd", [P, TT], F32)
        nt1 = sb("nt1", [P, TT], F32)
        nt2 = sb("nt2", [P, TT], F32)
        shifted = sb("shifted", [P, TT, E], F32)
        powers = sb("powers", [P, TT, E], F32)
        top = sb("top", [P, TT], F32)
        total = sb("total", [P, TT], F32)
        rt1 = sb("rt1", [P, ROPE_TILES, NH, HD], BF16)
        rt2 = sb("rt2", [P, ROPE_TILES, NH, HD], BF16)
        credit = sb("credit", [P, 2], F32)
        dve_scratch = sb("dve_scratch", [P, 1], F32)
        pool_scratch = sb("pool_scratch", [P, 1], F32)

        ring = [ctx.enter_context(nc.psum_tensor(f"ring{i}", [P, 2, 512], F32)) for i in range(2)]
        st_bank = [ctx.enter_context(nc.psum_tensor(f"st{i}", [P, 512], F32)) for i in range(ST_BANKS)]
        pv_bank = ctx.enter_context(nc.psum_tensor("pv", [P, 512], F32))

        ident_in = sem("ident_in")
        const_in = sem("const_in")
        w_in = sem("w_in")
        xa_in = sem("xa_in")
        xr_in = sem("xr_in")
        x1_out = sem("x1_out")
        xn2_ready = sem("xn2_ready")
        xn2_out = sem("xn2_out")
        wh_ready = sem("wh_ready")
        wl_ready = sem("wl_ready")
        high_ready = sem("high_ready")
        split_ready = sem("split_ready")
        shifted_ready = sem("shifted_ready")
        powers_ready = sem("powers_ready")
        const_ready = sem("const_ready")
        fills = sem("fills")
        bias_added = sem("bias_added")
        xn_ready = sem("xn_ready")
        ring_full = sem("ring_full")
        vector_freed = sem("vector_freed")
        scalar_freed = sem("scalar_freed")
        rope_done = sem("rope_done")
        qm_in = sem("qm_in")
        nm_ready = sem("nm_ready")
        nm_in = sem("nm_in")
        st_full = sem("st_full")
        st_free = sem("st_free")
        pv_done = sem("pv_done")
        ot_ready = sem("ot_ready")
        dve_own = sem("dve_own")
        pool_own = sem("pool_own")

        N_CONST = 6

        block = ctx.enter_context(nc.Block())

        @block.sync
        def _(sp):
            def rows(name, b):
                return d[name][bass.ds(b * T, T), :].rearrange("(i p) h -> p i h", p=P)

            sp.dma_start(XA[:], rows("x", 0)).then_inc(xa_in, 16)
            sp.dma_start(ident[:], d["ident"]).then_inc(ident_in, 16)
            for n, name in enumerate(("wq", "wk", "wv", "wo")):
                sp.dma_start(W_raw[:, :, H * n:H * n + H], d[name].rearrange("(k p) n -> p k n", p=P)).then_inc(w_in, 16)
            sp.dma_start(b_q[:], d["bq"].partition_broadcast(P)).then_inc(const_in, 16)
            sp.dma_start(b_v[:], d["bv"].partition_broadcast(P)).then_inc(const_in, 16)
            sp.dma_start(b_o[:], d["bo"].partition_broadcast(P)).then_inc(const_in, 16)
            sp.dma_start(cs_in[:, 0], d["cos"].rearrange("(i p) h -> p i h", p=P)).then_inc(const_in, 16)
            sp.dma_start(cs_in[:, 1], d["sin"].rearrange("(i p) h -> p i h", p=P)).then_inc(const_in, 16)
            sp.dma_start(gw[:], d["gwT"].rearrange("(k p) e -> p k e", p=P)).then_inc(const_in, 16)

            def load_heads(grp, after):
                sp.wait_ge(vector_freed, after)
                for j in range(4):
                    r = slice(QUAD * j, QUAD * j + QUAD)
                    sp.dma_start(QM[grp % G][j][r, :], QS[r, :]).then_inc(qm_in, 16)

            def load_maxima(grp, after):
                sp.wait_ge(vector_freed, after)
                for j in range(4):
                    sp.dma_start(QM[grp % G][j][QUAD * j + HD:QUAD * j + HD + 3, :],
                                 NS[3 * j:3 * j + 3, :]).then_inc(nm_in, 16)

            sp.wait_ge(fills, 4 * G)
            pro = Turn("prologue")
            load_heads(0, pro.vector_done(("qkT", 0)))
            load_heads(1, pro.vector_done(("qkT", 1)))
            load_maxima(0, pro.vector_done(("nm", 0)))

            def store_x1(b):
                sp.dma_start(rows("out", b), XR[:]).then_inc(x1_out, 16)

            def store_xn2(b):
                sp.wait_ge(xn2_ready, TT * (b + 1))
                sp.dma_start(rows("xn2", b), XN2[:]).then_inc(xn2_out, 16)

            def turn(b, prev, more):
                t = Turn(b, prev, more)
                if more:
                    sp.wait_ge(xn_ready, TT * (b + 1))
                    sp.dma_start(XA[:], rows("x", b + 1)).then_inc(xa_in, 16)
                for g, steps in enumerate(t.slots):
                    if g == 2:
                        if prev:
                            store_xn2(b - 1)
                            sp.wait_ge(x1_out, 16 * b)
                        sp.dma_start(XR[:], rows("x", b)).then_inc(xr_in, 16)
                    for item in [i for st in steps for i in st]:
                        if item[0] == "qkT":
                            load_heads(item[1], t.vector_done(item))
                        if item[0] == "nm":
                            load_maxima(item[1], t.vector_done(item))
                        if item == ("proj", 1):
                            sp.wait_ge(vector_freed, t.vector_done(item))
                            store_x1(b - 1)

            turns(sp, turn)
            sp.wait_ge(vector_freed, Turn("tail").vector_done(("proj", 1)))
            store_x1(B - 1)
            store_xn2(B - 1)
            sp.wait_ge(x1_out, 16 * B)
            sp.wait_ge(xn2_out, 16 * B)
            sp.wait_ge(nm_in, 64 * G * B)

        @block.gpsimd
        def _(pool):
            own = Tally(pool_own)
            for tiles in QM:
                for t in tiles:
                    nc.gpsimd.memset(t[:], 0.0).then_inc(fills, 1)
            own.inc(nc.gpsimd.memset(VA[:], 0.0))
            own.wait(pool)
            nc.gpsimd.memset(VA[:, :, :, HD:HD + 1], 1.0).then_inc(fills, 1)

            def settle():
                nc.gpsimd.tensor_tensor(pool_scratch[:], ident[:, 0:1], ident[:, 0:1], ALU.mult)

            def add_bias(b):
                pool.wait_ge(xr_in, 16 * (b + 1))
                nc.gpsimd.tensor_tensor(XR[:], XR[:], b_o[:].unsqueeze(1).to_broadcast([P, TT, H]),
                                        ALU.add).then_inc(bias_added, 1)

            def rope(b, own, after):
                pool.wait_ge(vector_freed, after)
                for n, A in enumerate((QP, KP)):
                    if n:
                        pool.wait_ge(rope_done, 2 * b + 1)
                    a = A[:, TT - ROPE_TILES:TT, :, 0:HD]
                    h = HD // 2

                    def over(c, lo, hi):
                        return c[:, :, lo:hi].unsqueeze(2).to_broadcast([P, ROPE_TILES, NH, hi - lo])
                    nc.gpsimd.tensor_tensor(rt1[:], a, over(cosb, 0, HD), ALU.mult)
                    nc.gpsimd.tensor_tensor(rt2[:, :, :, 0:h], a[:, :, :, h:HD], over(sinb, 0, h), ALU.mult)
                    own.inc(nc.gpsimd.tensor_tensor(rt2[:, :, :, h:HD], a[:, :, :, 0:h], over(sinb, h, HD), ALU.mult))
                    own.wait(pool)
                    nc.gpsimd.tensor_tensor(a, rt1[:], rt2[:], ALU.add).then_inc(rope_done, 1)

            ROPE_INCS = 2

            def negated_maxima(grp, own, after):
                pool.wait_ge(vector_freed, after)
                settle()
                m = MX[:, grp % 2]
                part = [NM[:, :, :, n].rearrange("p t j -> p j t") for n in range(3)]
                own.inc(nc.gpsimd.tensor_scalar(nmr[:], m, -1.0, None, ALU.mult))
                for n in range(2):
                    own.wait(pool)
                    settle()
                    own.inc(nc.gpsimd.tensor_copy(part[n], nmr[:]))
                    own.wait(pool)
                    own.inc(nc.gpsimd.tensor_tensor(nmr[:], nmr[:], part[n], ALU.subtract))
                own.wait(pool)
                settle()
                nc.gpsimd.tensor_copy(part[2], nmr[:]).then_inc(nm_ready, 1)

            NM_INCS = 5

            def split(t, item, own):
                hi, lo = (XH, XL) if item[0] == "xt" else (AH, AL)
                c = slice(512 * item[1], 512 * item[1] + 512)
                pool.wait_ge(scalar_freed, t.upto(item, "scalar"))
                settle()
                own.inc(nc.gpsimd.tensor_copy(hi[:, :, c], XT[:, :, c]))
                own.wait(pool)
                nc.gpsimd.tensor_tensor(lo[:, :, c], XT[:, :, c], hi[:, :, c].bitcast(F32),
                                        ALU.subtract).then_inc(split_ready, 1)

            SPLIT_INCS = 1

            pool.wait_ge(ident_in, 16)
            pool.wait_ge(const_in, 16 * N_CONST)
            pool.wait_ge(const_ready, 1)
            pro = Turn("prologue")
            rope(0, own, pro.vector_done(("qk", 3, 0)))
            negated_maxima(0, own, pro.vector_done(("sc", 0, 3, TT - 1)))
            HEAD = own.n
            PER_FIRST = ROPE_INCS + G * NM_INCS + 2 * SPLIT_INCS
            PER = PER_FIRST + 2 * SPLIT_INCS
            assert HEAD == 1 + ROPE_INCS + NM_INCS

            def turn(b, prev, more):
                t = Turn(b, prev, more)
                own = Tally(pool_own, HEAD + (PER_FIRST + (b - 1) * PER if prev else 0))
                for g in range(G):
                    for item in [i for st in t.slots[g] for i in st if split_late(i)]:
                        split(t, item, own)
                    if g == 2 and more:
                        rope(b + 1, own, t.vector_done(("qk", 3, 1)))
                    if g == G - 1:
                        add_bias(b)
                    if more or g < G - 1:
                        negated_maxima(g + 1, own, t.vector_done(("sc", g + 1, 3, TT - 1)))
                assert not more or own.n == (PER if prev else PER_FIRST)

            turns(pool, turn)
            own = Tally(pool_own, HEAD + PER_FIRST + (B - 2) * PER + PER - ROPE_INCS - NM_INCS - 2 * SPLIT_INCS)
            for item in TAIL[1:3]:
                split(Turn("tail"), item, own)

        @block.vector
        def _(dve):
            own = Tally(dve_own)
            for A in (QP, KP):
                own.inc(nc.vector.memset(A[:], 0.0))
            own.wait(dve)
            nc.vector.memset(KP[:, :, :, HD:HD + 3], 1.0)

            def settle():
                nc.vector.memset(dve_scratch[:], 0.0)

            def x1_stands(after, own):
                own.wait(dve)
                dve.wait_ge(vector_freed, after)
                settle()

            def statistics(src, tiles, own):
                for i in tiles:
                    own.inc(nc.vector.bn_stats(stats[:, i, :], src[:, i, :]))
                own.wait(dve)
                settle()
                for i in tiles:
                    own.inc(nc.vector.bn_aggr(mv[:, i, :], stats[:, i, :]))

            def normalise_step(k, out, src, ready, own):
                own.wait(dve)
                if k < RSQRT_STEPS:
                    own.inc(rsqrt_step(nc, k, rstd[:], nt1[:], nt2[:], mv[:, :, 1]))
                    return
                for i in range(2 * (k - RSQRT_STEPS), 2 * (k - RSQRT_STEPS) + 2):
                    nc.vector.tensor_scalar(out[:, i, :], src[:, i, :], mv[:, i, 0:1], rstd[:, i:i + 1],
                                            ALU.subtract, ALU.mult).then_inc(ready, 1)

            NORMALISE_STEPS = RSQRT_STEPS + TT // 2

            def xn2_stored(b, own):
                if not (isinstance(b, int) and b == 0):
                    own.wait(dve)
                    dve.wait_ge(xn2_out, 16 * b)
                    settle()

            def finish_gates(b, own):
                dve.wait_ge(powers_ready, b + 1)
                own.inc(nc.vector.reduce_sum(total[:], powers[:], AX.X))
                own.wait(dve)
                own.inc(nc.vector.reciprocal(total[:], total[:]))
                own.wait(dve)
                own.inc(nc.vector.tensor_tensor(SC[:, :, bass.ds(b * E, E)], powers[:],
                                                total[:].unsqueeze(2).to_broadcast([P, TT, E]), ALU.mult))
                own.wait(dve)

            LN_INCS = 2 * TT + RSQRT_STEPS
            GATE_INCS = 3 + 2
            OT_INCS = 1

            def consume(item, t, b, own):
                dve.wait_ge(ring_full, t.upto(item))
                R = ring[t.pair(item)]
                kind = item[0]
                if kind == "xt":
                    c = slice(512 * item[1], 512 * item[1] + 512)
                    dve.wait_ge(high_ready, item[1] + 1)
                    out = nc.vector.tensor_tensor(XL[:, :, c], R[:], XH[:, :, c].bitcast(F32), ALU.subtract)
                elif kind == "qk":
                    tiles = slice(2 * item[1], 2 * item[1] + 2)
                    nc.vector.tensor_tensor(
                        QP[:, tiles, :, 0:HD], R[:, :, 0:H].rearrange("p t (h c) -> p t h c", c=HD),
                        b_q[:].rearrange("p (h c) -> p h c", c=HD).unsqueeze(1).to_broadcast([P, 2, NH, HD]), ALU.add)
                    out = nc.vector.tensor_copy(KP[:, tiles, :, 0:HD],
                                                R[:, :, H:2 * H].rearrange("p t (h c) -> p t h c", c=HD))
                elif kind == "qkT":
                    n = G * b + item[1]
                    if not (isinstance(n, int) and n == 0):
                        dve.wait_ge(qm_in, 64 * n)
                    nc.vector.tensor_copy(KT[item[1] % G][:], R[:, 1, :].bitcast(BF16))
                    out = nc.vector.tensor_copy(QS[:], R[:, 0, :].bitcast(BF16))
                elif kind == "v":
                    if t.kind == "prologue":
                        dve.wait_ge(fills, 4 * G + 1)
                    for half in range(2):
                        tiles = slice(4 * item[1] + 2 * half, 4 * item[1] + 2 * half + 2)
                        out = nc.vector.tensor_tensor(
                            VA[:, tiles, :, 0:HD], R[:, half, :].rearrange("p (t h c) -> p t h c", t=2, c=HD),
                            b_v[:].rearrange("p (h c) -> p h c", c=HD).unsqueeze(1).to_broadcast([P, 2, NH, HD]),
                            ALU.add)
                elif kind == "sc":
                    _, grp, j, qt = item
                    out = nc.vector.reduce_max(MX[:, grp % 2, j, qt:qt + 1], R[:], AX.XY)
                elif kind == "nm":
                    n = G * b + item[1]
                    if not (isinstance(n, int) and n == 0):
                        dve.wait_ge(nm_in, 64 * n)
                    out = nc.vector.tensor_copy(NS[:], R[0:12, 0, :].bitcast(BF16))
                elif kind == "ot":
                    _, g, qh = item
                    g %= G
                    o = R[:, 0, :].rearrange("p (t j c) -> p t j c", t=4, c=QUAD)
                    own.inc(nc.vector.reciprocal(RD[:, qh], o[:, :, :, HD]))
                    own.wait(dve)
                    out = nc.vector.tensor_tensor(
                        AO[:, 4 * qh:4 * qh + 4, 64 * g:64 * g + 64].rearrange("p t (j c) -> p t j c", c=HD),
                        o[:, :, :, 0:HD], RD[:, qh].unsqueeze(3).to_broadcast([P, 4, 4, HD]), ALU.mult)
                elif kind == "lg":
                    tiles = slice(4 * item[1], 4 * item[1] + 4)
                    logits = R[:, 0, 0:4 * E].rearrange("p (t e) -> p t e", e=E)
                    own.inc(nc.vector.reduce_max(top[:, tiles], logits, AX.X))
                    own.wait(dve)
                    out = nc.vector.tensor_tensor(shifted[:, tiles, :], logits, top[:, tiles].unsqueeze(2).to_broadcast([P, 4, E]),
                                                  ALU.subtract)
                elif kind == "proj":
                    x = XR[:, 4 * item[1]:4 * item[1] + 4, :]
                    dve.wait_ge(bias_added, b)
                    out = nc.vector.tensor_tensor(x, R[:].rearrange("p a (c n) -> p (a c) n", n=H), x, ALU.add)
                out.then_inc(vector_freed, 1)

            dve.wait_ge(xa_in, 16)
            statistics(XA, range(TT), own)
            for k in range(NORMALISE_STEPS):
                normalise_step(k, XN, XA, xn_ready, own)
            dve.wait_ge(wh_ready, 1)
            nc.vector.tensor_tensor(WL[:], W_raw[:], WH[:].bitcast(F32), ALU.subtract).then_inc(wl_ready, 1)
            dve.wait_ge(ident_in, 16)
            nc.vector.tensor_copy(identb[:], ident[:])
            dve.wait_ge(const_in, 16 * N_CONST)
            nc.vector.tensor_copy(cosb[:], cs_in[:, 0])
            own.inc(nc.vector.tensor_copy(sinb[:], cs_in[:, 1]))
            own.wait(dve)
            nc.vector.tensor_scalar(sinb[:, :, 0:HD // 2], sinb[:, :, 0:HD // 2], -1.0, None,
                                    ALU.mult).then_inc(const_ready, 1)
            for item in PRO:
                consume(item, Turn("prologue"), 0, own)
            HEAD = own.n
            PER_FIRST = LN_INCS + (2 * G - 1) * OT_INCS
            PER = PER_FIRST + LN_INCS + GATE_INCS + OT_INCS

            def turn(b, prev, more):
                t = Turn(b, prev, more)
                own = Tally(dve_own, HEAD + (PER_FIRST + (b - 1) * PER if prev else 0))
                next_steps = x1_steps = 0
                for g in range(G):
                    for s in range(STEPS):
                        for item in t.slots[g][s]:
                            if not by_scalar(item):
                                consume(item, t, b, own)
                            if more and g * STEPS + s >= 7 and next_steps < NORMALISE_STEPS:
                                normalise_step(next_steps, XN, XA, xn_ready, own)
                                next_steps += 1
                            if prev and g * STEPS + s >= STEPS + 5 and x1_steps < NORMALISE_STEPS:
                                if x1_steps == 0:
                                    xn2_stored(b - 1, own)
                                normalise_step(x1_steps, XN2, XR, xn2_ready, own)
                                x1_steps += 1
                        if more and g == 0:
                            if s == 1:
                                own.wait(dve)
                                dve.wait_ge(xa_in, 16 * (b + 2))
                                settle()
                            if s in (1, 3, 5, 6):
                                n = (1, 3, 5, 6).index(s)
                                statistics(XA, (2 * n, 2 * n + 1), own)
                        if prev and g == 1:
                            if s == 1:
                                x1_stands(t.vector_done(("proj", 1)), own)
                            if s in (1, 2, 3, 4):
                                statistics(XR, (2 * (s - 1), 2 * (s - 1) + 1), own)
                        if prev and (g, s) == (3, 9):
                            finish_gates(b - 1, own)
                for item in t.flush:
                    consume(item, t, b, own)
                if more:
                    assert own.n == (PER if prev else PER_FIRST), (own.n, PER, PER_FIRST)

            turns(dve, turn)
            own = Tally(dve_own, HEAD + PER_FIRST + (B - 2) * PER + PER - LN_INCS)
            tail = Turn("tail")
            for item in TAIL[:5]:
                if not by_scalar(item):
                    consume(item, tail, B, own)
            x1_stands(tail.vector_done(("proj", 1)), own)
            statistics(XR, range(TT), own)
            xn2_stored(B - 1, own)
            for k in range(NORMALISE_STEPS):
                normalise_step(k, XN2, XR, xn2_ready, own)
            for item in TAIL[5:]:
                if not by_scalar(item):
                    consume(item, tail, B, own)
            finish_gates(B - 1, own)

        @block.scalar
        def _(act):
            act.wait_ge(w_in, 64)
            nc.scalar.copy(WH[:], W_raw[:]).then_inc(wh_ready, 1)
            act.wait_ge(ident_in, 16)
            nc.scalar.activation(credit[:, 0:1], ident[:, 0:1], ACT.Exp).then_inc(st_free, ST_BANKS)
            nc.scalar.activation(credit[:, 1:2], ident[:, 0:1], ACT.Exp).then_inc(ot_ready, 1)

            def evacuate(b, half):
                act.wait_ge(pv_done, G * STEPS * b + TT * (half + 1) + P_STEPS)
                nc.scalar.copy(OT[:], pv_bank[:]).then_inc(ot_ready, 1)

            def high_parts(item, t):
                act.wait_ge(ring_full, t.upto(item))
                nc.scalar.copy(XH[:, :, 512 * item[1]:512 * item[1] + 512], ring[t.pair(item)][:]).then_inc(high_ready, 1)

            def empty(item, t):
                splits = t.upto(item, "split") - (2 if split_late(item) else 0)
                if not (isinstance(splits, int) and splits <= 0):
                    act.wait_ge(split_ready, splits)
                act.wait_ge(ring_full, t.upto(item))
                nc.scalar.copy(XT[:, :, 512 * item[1]:512 * item[1] + 512], ring[t.pair(item)][:]).then_inc(scalar_freed, 1)

            def gate_powers(b, after):
                act.wait_ge(vector_freed, after)
                nc.scalar.activation(powers[:], shifted[:], ACT.Exp).then_inc(powers_ready, 1)

            for item in PRO[:2]:
                high_parts(item, Turn("prologue"))

            def turn(b, prev, more):
                t = Turn(b, prev, more)
                for g in range(G):
                    for s in range(STEPS):
                        step = g * STEPS + s
                        items = t.slots[g][s]
                        cut = (len(items) + 1) // 2
                        for j in range(4):
                            n = 4 * step + j
                            if j == 0:
                                act.wait_ge(pv_done, G * STEPS * b + step + 1)
                            act.wait_ge(st_full, 4 * G * STEPS * b + n + 1)
                            nc.scalar.activation(PR[step % P_STEPS][:, j, :], st_bank[n % ST_BANKS][:], ACT.Exp,
                                                 scale=0.25).then_inc(st_free, 1)
                            if j == 0 and s % TT == 1 and (prev or step > 1):
                                half = step // TT - 1
                                if half == -1:
                                    act.wait_ge(ring_full, t.before())
                                elif half == 0:
                                    act.wait_ge(ring_full, t.upto(("ot", -1, 1)) if prev else t.before())
                                else:
                                    act.wait_ge(ring_full, t.upto(("ot", (half - 1) // 2, (half - 1) % 2)))
                                evacuate(b, half)
                            for item in items[:cut] if j == 2 else items[cut:] if j == 3 else []:
                                if by_scalar(item):
                                    empty(item, t)
                        if prev and (g, s) == (3, 7):
                            gate_powers(b - 1, t.vector_done(("lg", 1)))

            turns(act, turn)
            tail = Turn("tail")
            act.wait_ge(ring_full, tail.before())
            evacuate(B, -1)
            for item in TAIL:
                if by_scalar(item):
                    empty(item, tail)
            gate_powers(B - 1, tail.vector_done(("lg", 1)))

        @block.tensor
        def _(pe):
            pe.wait_ge(ident_in, 16)

            def fill(item, t, b):
                n = t.order.index(item)
                if n >= 2 and by_scalar(t.order[n - 2]):
                    pe.wait_ge(scalar_freed, t.upto(t.order[n - 2], "scalar"))
                elif n >= 2:
                    pe.wait_ge(vector_freed, t.vector_done(t.order[n - 2]))
                elif t.kind != "prologue":
                    pe.wait_ge(vector_freed, t.before("vector") + n - 1)
                R = ring[t.pair(item)]
                kind = item[0]
                if kind == "xt":
                    if item[1] == 0:
                        pe.wait_ge(xn_ready, TT * (b + item[2] + 1))
                    for h in range(KH):
                        for m in range(4):
                            out = nc.tensor.transpose(R[:, h, P * m:P * m + P],
                                                      XN[:, 4 * item[1] + m, P * h:P * h + P], ident[:])
                elif kind == "qk":
                    if item == ("qk", 3, 0):
                        pe.wait_ge(wl_ready, 1)
                        pe.wait_ge(vector_freed, t.vector_done(("xt", 1, 0)))
                    elif item == ("qk", 0, 1):
                        pe.wait_ge(split_ready, t.upto(("xt", 1, 1), "split"))
                    for m in range(2):
                        i = 2 * item[1] + m
                        for h in range(KH):
                            out = three(nc, R[:, m, :], (XH, WH), (XL, WL), (slice(None), h, slice(P * i, P * i + P)),
                                        (slice(None), h, slice(0, 2 * H)), h == 0, h == KH - 1)
                elif kind == "v":
                    for m in range(4):
                        i = 4 * item[1] + m
                        for h in range(KH):
                            out = three(nc, R[:, m // 2, H * (m % 2):H * (m % 2) + H], (XH, WH), (XL, WL),
                                        (slice(None), h, slice(P * i, P * i + P)),
                                        (slice(None), h, slice(2 * H, 3 * H)), h == 0, h == KH - 1)
                elif kind == "qkT":
                    g = item[1] % G
                    if t.kind == "prologue":
                        pe.wait_ge(vector_freed, t.vector_done(("qk", 2, 0)))
                        pe.wait_ge(const_ready, 1)
                    pe.wait_ge(rope_done, 2 * (b + item[1] // G + 1))
                    for n, A in enumerate((QP, KP)):
                        for m in range(TT):
                            out = nc.tensor.transpose(
                                R[:, n, :].bitcast(BF16)[:, P * m:P * m + P],
                                A[:, m, 4 * g:4 * g + 4, :].rearrange("p h c -> p (h c)"), identb[:])
                elif kind == "sc":
                    _, grp, j, qt = item
                    if j == 0 and qt == 0:
                        pe.wait_ge(qm_in, 64 * (G * b + grp + 1))
                    for n in range(2):
                        out = nc.tensor.matmul(R[:, n, :], QM[grp % G][j][:, P * qt:P * qt + P],
                                               KT[grp % G][:, 512 * n:512 * n + 512], start=True, stop=True)
                elif kind == "nm":
                    pe.wait_ge(nm_ready, G * b + item[1] + 1)
                    for m in range(TT):
                        out = nc.tensor.transpose(R[0:12, 0, :].bitcast(BF16)[:, P * m:P * m + P],
                                                  NM[:, m].rearrange("p j n -> p (j n)"), identb[:])
                elif kind == "ot":
                    _, g, qh = item
                    pe.wait_ge(ot_ready, 2 * G * b + 2 * g + qh + 2)
                    for m in range(4):
                        out = nc.tensor.transpose(R[:, 0, P * m:P * m + P], OT[:, P * m:P * m + P], ident[:])
                elif kind == "aot":
                    pe.wait_ge(vector_freed, t.vector_done(("ot", -1, 1)))
                    for h in range(KH):
                        for m in range(4):
                            out = nc.tensor.transpose(R[:, h, P * m:P * m + P],
                                                      AO[:, 4 * item[1] + m, P * h:P * h + P], ident[:])
                elif kind == "proj":
                    pe.wait_ge(split_ready, t.upto(("aot", item[1]), "split"))
                    for m in range(4):
                        i = 4 * item[1] + m
                        for h in range(KH):
                            out = three(nc, R[:, m // 2, H * (m % 2):H * (m % 2) + H], (AH, WH), (AL, WL),
                                        (slice(None), h, slice(P * i, P * i + P)),
                                        (slice(None), h, slice(3 * H, 4 * H)), h == 0, h == KH - 1)
                elif kind == "x2t":
                    pe.wait_ge(xn2_ready, TT * b)
                    for h in range(KH):
                        for m in range(4):
                            out = nc.tensor.transpose(R[:, h, P * m:P * m + P],
                                                      XN2[:, 4 * item[1] + m, P * h:P * h + P], ident[:])
                elif kind == "lg":
                    pe.wait_ge(scalar_freed, t.upto(("x2t", item[1]), "scalar"))
                    for m in range(4):
                        i = 4 * item[1] + m
                        for h in range(KH):
                            out = nc.tensor.matmul(R[:, 0, E * m:E * m + E], XT[:, h, P * i:P * i + P], gw[:, h, :],
                                                   start=(h == 0), stop=(h == KH - 1))
                out.then_inc(ring_full, 1)

            for item in PRO:
                fill(item, Turn("prologue"), 0)
            nc.tensor.matmul(pv_bank[:, 0:P], identb[:], identb[:], start=True, stop=True).then_inc(pv_done, P_STEPS)

            def score_bank(b, g, s, j):
                n = 4 * (g * STEPS + s) + j
                back = {0: 0, 1: -2, 2: -1}.get(n, n - 2)
                pe.wait_ge(st_free, 4 * G * STEPS * b + ST_BANKS + back)
                qh, kt = s // TT, s % TT
                nc.tensor.matmul(st_bank[n % ST_BANKS][:], KT[g][:, P * kt:P * kt + P],
                                 QM[g][j][:, 512 * qh:512 * qh + 512], start=True, stop=True).then_inc(st_full, 1)

            def weigh_values(t, b, g, s):
                step = g * STEPS + s
                kt = s % TT
                if kt == 0:
                    pe.wait_ge(ot_ready, 2 * G * b + step // TT + 1)
                    if step == 0:
                        pe.wait_ge(vector_freed, t.before("vector"))
                pe.wait_ge(st_free, 4 * G * STEPS * b + 4 * (step + 1) + ST_BANKS)
                for j in range(4):
                    out = nc.tensor.matmul(pv_bank[QUAD * j:QUAD * j + QUAD, :], VA[:, kt, 4 * g + j, :],
                                           PR[step % P_STEPS][:, j, :], start=(kt == 0), stop=(kt == TT - 1))
                return out

            def finish_step(t, b, step):
                weigh_values(t, b, step // STEPS, step % STEPS).then_inc(pv_done, 1)

            def turn(b, prev, more):
                t = Turn(b, prev, more)
                for g in range(G):
                    pe.wait_ge(nm_in, 64 * (G * b + g + 1))
                    for s in range(STEPS):
                        items = t.slots[g][s]
                        cut = (len(items) + 1) // 2
                        for j in range(3):
                            score_bank(b, g, s, j)
                        for item in items[:cut]:
                            fill(item, t, b)
                        score_bank(b, g, s, 3)
                        if g or s:
                            finish_step(t, b, g * STEPS + s - 1)
                        for item in items[cut:]:
                            fill(item, t, b)
                finish_step(t, b, G * STEPS - 1)
                for item in t.flush:
                    fill(item, t, b)

            turns(pe, turn)
            for item in TAIL:
                fill(item, Turn("tail"), B)



KD, KF = D // P, F // P
CAP = 128


def feed_forward(nc, d, SC, WT, IX, B, shared):
    T = 1024
    TT = T // P
    BE = B * E
    CT = 4 if shared else B // 2
    N = CT * P
    HALVES = 2
    K = HALVES if shared else 2 * HALVES
    R = B if shared else E // 2
    ROUNDS = CAP // 8
    tag = "sh_" if shared else "ex_"
    ctx = ExitStack()
    with ctx:
        def sb(name, shape, dt):
            return ctx.enter_context(nc.sbuf_tensor(tag + name, shape, dt))

        def sem(name):
            return ctx.enter_context(nc.semaphore(tag + name))

        ident = sb("ident", [P, P], F32)
        W = [sb("Wg", [P, KD, F], F32), sb("Wu", [P, KD, F], F32), sb("Wd", [P, KF, D], F32)]
        SETS = 1 if shared else 2
        WH = [[sb(f"WH{q}{i}", list(w.shape), FR) for i, w in enumerate(W)] for q in range(SETS)]
        WL = [[sb(f"WL{q}{i}", list(w.shape), FR) for i, w in enumerate(W)] for q in range(SETS)]
        XG = [sb(f"XG{c}", [P, CT, D], F32) for c in range(2)]
        XH = [sb(f"XH{c}", [P, KD, N], FR) for c in range(2)]
        XL = [sb(f"XL{c}", [P, KD, N], FR) for c in range(2)]
        GL = [sb(f"GL{c}", [P, N], F32) for c in range(2)]
        HF = [sb(f"HF{c}", [P, N], F32) for c in range(2)]
        HH = [sb(f"HH{c}", [P, KF, N], FR) for c in range(2)]
        HL = [sb(f"HL{c}", [P, KF, N], FR) for c in range(2)]
        YS = [sb(f"YS{c}", [P, CT, D], F32) for c in range(2)]
        if shared:
            X1 = [sb(f"X1{c}", [P, CT, D], F32) for c in range(2)]
            sct = sb("sct", [BE, T], F32)
            vals = sb("vals", [BE, CAP], F32)
            inds = sb("inds", [BE, CAP], U32)
            indf = sb("indf", [BE, CAP], F32)
            row0 = sb("row0", [BE, 1], F32)
            v8 = sb("v8", [BE, 8], F32)
            i8 = sb("i8", [BE, 8], U32)
            dve_scratch = sb("dve_scratch", [P, 1], F32)
        else:
            rows_in = sb("rows_in", [P, B], U32)
            rows_out = sb("rows_out", [P, B], U32)
            WC = [sb(f"WC{q}", [P, B], F32) for q in range(2)]
            pool_scratch = sb("pool_scratch", [P, 1], F32)

        gu = [ctx.enter_context(nc.psum_tensor(f"{tag}gu{i}", [P, 2, 512], F32)) for i in range(2)]
        turned = ctx.enter_context(nc.psum_tensor(f"{tag}turned", [P, KD, 512], F32))
        y = ctx.enter_context(nc.psum_tensor(f"{tag}y", [P, 2, 512], F32))

        const_in = sem("const_in")
        w_in = sem("w_in")
        wh_ready = sem("wh_ready")
        wl_ready = sem("wl_ready")
        x_in = [sem(f"x_in{c}") for c in range(2)]
        x1_in = [sem(f"x1_in{c}") for c in range(2)]
        turned_full = sem("turned_full")
        xh_ready = sem("xh_ready")
        xl_ready = sem("xl_ready")
        gu_full = sem("gu_full")
        gelu_ready = sem("gelu_ready")
        hf_ready = sem("hf_ready")
        hh_ready = sem("hh_ready")
        hl_ready = sem("hl_ready")
        y_full = sem("y_full")
        ys_ready = sem("ys_ready")
        y_out = [sem(f"y_out{c}") for c in range(2)]
        ic_ready = sem("ic_ready")
        oc_ready = sem("oc_ready")
        wc_ready = sem("wc_ready")
        settled = sem("settled")
        sct_full = sem("sct_full")
        sct_ready = sem("sct_ready")
        sel_ready = sem("sel_ready")
        sel_full = sem("sel_full")
        sel_done = sem("sel_done")
        own_sem = sem("own")

        block = ctx.enter_context(nc.Block())

        def groups(engine, body):
            body(0, True, R == 1)
            if R > 2:
                with engine.Fori(1, R - 1) as r:
                    body(r, False, False)
            if R > 1:
                body(R - 1, False, True)

        Y_INC = CT if not shared else 1
        X_INC = 16 if shared else 16 * CT

        def expert(r, k):
            return 2 * r + k // HALVES

        def load_weights(sp, e):
            if shared:
                src = [d["SgT"], d["SuT"], d["SdT"]]
            else:
                src = [d["WgT"][bass.ds(e * D, D), :], d["WuT"][bass.ds(e * D, D), :], d["WdT"][bass.ds(e * F, F), :]]
            for w, s in zip(W, src):
                sp.dma_start(w[:], s.rearrange("(k p) n -> p k n", p=P)).then_inc(w_in, 16)

        @block.sync
        def _(sp):
            sp.dma_start(ident[:], d["ident"]).then_inc(const_in, 16)
            if shared:
                sp.dma_start(row0[:], d["row0"][0:BE, :]).then_inc(const_in, 16)
                load_weights(sp, 0)

                def rows(name, n):
                    return d[name][bass.ds(n * N, N), :].rearrange("(i p) h -> p i h", p=P)

                def load(r, k):
                    n = r * K + k
                    if not (isinstance(n, int) and n < 2):
                        sp.wait_ge(turned_full, n - 1)
                    sp.dma_start(XG[k % 2][:], rows("xn2", n)).then_inc(x_in[k % 2], 16)

                def load_x1(r, k):
                    n = r * K + k
                    if not (isinstance(n, int) and n < 2):
                        sp.wait_ge(ys_ready, n - 1)
                    sp.dma_start(X1[k % 2][:], rows("out", n)).then_inc(x1_in[k % 2], 16)

                def store(r, k):
                    n = r * K + k
                    sp.wait_ge(ys_ready, n + 1)
                    sp.dma_start(rows("out", n), YS[k % 2][:]).then_inc(y_out[k % 2], 16)
                load(0, 0)
                load(0, 1)
                load_x1(0, 0)

                def group(r, first, last):
                    for k in range(K):
                        if not (last and k >= K - 2):
                            load(r if k < K - 2 else r + 1, (k + 2) % K)
                        if not (first and k == 0):
                            store(r if k else r - 1, (k - 1) % K)
                        if not (last and k == K - 1):
                            load_x1(r if k < K - 1 else r + 1, (k + 1) % K)
                groups(sp, group)
                store(R - 1, K - 1)
                for c in range(2):
                    sp.wait_ge(y_out[c], 16 * R * K // 2)
            else:
                load_weights(sp, 0)

                def load_next(e):
                    sp.wait_ge(wl_ready, 3 * (e + 1))
                    load_weights(sp, e + 1)
                load_next(0)
                if E > 2:
                    with sp.Fori(1, E - 1) as e:
                        load_next(e)

        @block.gpsimd
        def _(pool):
            if shared:
                return

            pool.wait_ge(const_in, 16)

            def settle(own):
                if not isinstance(own.base, int) or own.base + own.n > 0:
                    own.wait(pool)
                own.inc(nc.gpsimd.tensor_tensor(pool_scratch[:], ident[:, 0:1], ident[:, 0:1], ALU.mult))

            def take_rows(IC, e, own, taken):
                settle(own)
                nc.gpsimd.tensor_copy(IC[:], IX[:, :, bass.ds(e, 1)].rearrange("p b a -> p (b a)")
                                      ).then_inc(taken, 1)
                pool.wait_ge(taken, e + 1)

            def gather(r, k, own):
                n = r * K + k
                if k % HALVES == 0:
                    if not (isinstance(n, int) and n == 0):
                        for c in range(2):
                            pool.wait_ge(x_in[c], X_INC * expert(r, k))
                    take_rows(rows_in, expert(r, k), own, ic_ready)
                if not (isinstance(n, int) and n < 2):
                    pool.wait_ge(turned_full, n - 1)
                settle(own)
                for t in range(CT):
                    b = CT * (k % HALVES) + t
                    nc.gpsimd.indirect_dma_start(
                        out=XG[k % 2][:, t, :], out_offset=None, in_=d["xn2"],
                        in_offset=bass.IndirectOffsetOnAxis(ap=rows_in[:, b:b + 1], axis=0)).then_inc(x_in[k % 2], 16)

            def scatter(r, k, own):
                n = r * K + k
                e = expert(r, k)
                if k % HALVES == 0:
                    if not (isinstance(n, int) and n == 0):
                        for c in range(2):
                            pool.wait_ge(y_out[c], 16 * CT * e)
                    take_rows(rows_out, e, own, oc_ready)
                pool.wait_ge(ys_ready, Y_INC * (n + 1))
                if not (isinstance(e, int) and e == 0):
                    pool.wait_ge(y_out[k % 2], 16 * CT * e)
                settle(own)
                for t in range(CT):
                    b = CT * (k % HALVES) + t
                    nc.gpsimd.indirect_dma_start(
                        out=d["out"], out_offset=bass.IndirectOffsetOnAxis(ap=rows_out[:, b:b + 1], axis=0),
                        in_=YS[k % 2][:, t, :], in_offset=None, compute_op=ALU.add).then_inc(y_out[k % 2], 16)
            own = Tally(settled)
            gather(0, 0, own)
            gather(0, 1, own)
            HEAD = own.n
            PER = 2 * K + 2 * (K // HALVES)

            def group(r, first, last):
                own = Tally(settled, HEAD if first else HEAD + r * PER - 1)
                for k in range(K):
                    if not (last and k >= K - 2):
                        gather(r if k < K - 2 else r + 1, (k + 2) % K, own)
                    if not (first and k == 0):
                        scatter(r if k else r - 1, (k - 1) % K, own)
            groups(pool, group)
            own = Tally(settled, HEAD + R * PER - 1 - 3)
            scatter(R - 1, K - 1, own)
            for c in range(2):
                pool.wait_ge(y_out[c], 16 * CT * R * K // 2)

        @block.scalar
        def _(act):
            def split_weights(e, q, i):
                act.wait_ge(w_in, 48 * (e + 1))
                nc.scalar.copy(WH[q][i][:], W[i][:]).then_inc(wh_ready, 1)

            def split_tokens(r, k):
                n = r * K + k
                act.wait_ge(turned_full, n + 1)
                nc.scalar.copy(XH[k % 2][:], turned[:, :, 0:N]).then_inc(xh_ready, 1)

            def gelu(n, f):
                act.wait_ge(gu_full, KF * n + f + 1)
                nc.scalar.activation(GL[f % 2][:], gu[f % 2][:, 0, 0:N], ACT.Gelu).then_inc(gelu_ready, 1)

            def high(n, k, f):
                act.wait_ge(hf_ready, KF * n + f + 1)
                nc.scalar.copy(HH[k % 2][:, f, :], HF[f % 2][:]).then_inc(hh_ready, 1)

            split_weights(0, 0, 0)
            split_weights(0, 0, 1)
            split_tokens(0, 0)
            split_weights(0, 0, 2)

            def group(r, first, last):
                for k in range(K):
                    n = r * K + k
                    final = last and k == K - 1
                    more = not shared and not (last and k >= K - HALVES)
                    e, q = expert(r, k) + 1, (k // HALVES + 1) % 2
                    gelu(n, 0)
                    gelu(n, 1)
                    high(n, k, 0)
                    if not final:
                        split_tokens(r if k < K - 1 else r + 1, (k + 1) % K)
                    gelu(n, 2)
                    high(n, k, 1)
                    gelu(n, 3)
                    high(n, k, 2)
                    if more and k % HALVES == 0:
                        if not (isinstance(n, int) and n == 0):
                            act.wait_ge(y_full, n)
                        split_weights(e, q, 0)
                    if more and k % HALVES == 1:
                        split_weights(e, q, 2)
                    high(n, k, 3)
                    if more and k % HALVES == 0:
                        split_weights(e, q, 1)
            groups(act, group)

        @block.vector
        def _(dve):
            def split_weights(e, q, i):
                dve.wait_ge(wh_ready, 3 * e + i + 1)
                nc.vector.tensor_tensor(WL[q][i][:], W[i][:], WH[q][i][:].bitcast(F32),
                                        ALU.subtract).then_inc(wl_ready, 1)
                if not shared and i == 2:
                    if not (isinstance(e, int) and e < 2):
                        dve.wait_ge(ys_ready, Y_INC * HALVES * (e - 1))
                    nc.vector.tensor_copy(WC[q][:], WT[:, :, bass.ds(e, 1)].rearrange("p b a -> p (b a)")
                                          ).then_inc(wc_ready, 1)

            def split_tokens(r, k):
                n = r * K + k
                dve.wait_ge(xh_ready, n + 1)
                nc.vector.tensor_tensor(XL[k % 2][:], turned[:, :, 0:N], XH[k % 2][:].bitcast(F32),
                                        ALU.subtract).then_inc(xl_ready, 1)

            def product(n, f):
                i = KF * n + f
                if not (isinstance(i, int) and i < 2):
                    dve.wait_ge(hl_ready, i - 1)
                dve.wait_ge(gelu_ready, i + 1)
                nc.vector.tensor_tensor(HF[f % 2][:], GL[f % 2][:], gu[f % 2][:, 1, 0:N], ALU.mult).then_inc(hf_ready, 1)

            def low(n, k, f):
                dve.wait_ge(hh_ready, KF * n + f + 1)
                nc.vector.tensor_tensor(HL[k % 2][:, f, :], HF[f % 2][:], HH[k % 2][:, f, :].bitcast(F32),
                                        ALU.subtract).then_inc(hl_ready, 1)

            def result(r, k):
                n = r * K + k
                dve.wait_ge(y_full, n + 1)
                if not (isinstance(n, int) and n < 2):
                    dve.wait_ge(y_out[k % 2], X_INC * (r * (K // 2) + k // 2))
                yv = y[:].rearrange("p a (c n) -> p (a c) n", n=D)
                if shared:
                    dve.wait_ge(x1_in[k % 2], 16 * (r * (K // 2) + k // 2 + 1))
                    nc.vector.tensor_tensor(YS[k % 2][:], yv, X1[k % 2][:], ALU.add).then_inc(ys_ready, 1)
                else:
                    dve.wait_ge(wc_ready, expert(r, k) + 1)
                    for t in range(CT):
                        b = CT * (k % HALVES) + t
                        nc.vector.tensor_scalar(YS[k % 2][:, t, :], yv[:, t, :], WC[(k // HALVES) % 2][:, b:b + 1],
                                                None, ALU.mult).then_inc(ys_ready, 1)

            CHUNKS = R * K
            TURNS = -(-ROUNDS // CHUNKS)

            def select(s, part, own):
                own.wait(dve)
                if part == 0:
                    nc.vector.memset(dve_scratch[:], 0.0)
                    own.inc(nc.vector.max(v8[:], sct[:]))
                elif part == 1:
                    nc.vector.tensor_copy(vals[:, bass.ds(8 * s, 8)], v8[:])
                    own.inc(nc.vector.max_index(i8[:], v8[:], sct[:]))
                else:
                    nc.vector.tensor_copy(inds[:, bass.ds(8 * s, 8)], i8[:])
                    own.inc(nc.vector.match_replace(sct[:], v8[:], sct[:], -1.0))

            split_weights(0, 0, 0)
            split_weights(0, 0, 1)
            split_tokens(0, 0)
            split_weights(0, 0, 2)
            if shared:
                dve.wait_ge(sct_full, 1)
                nc.vector.tensor_copy(sct[:], y[0:BE].rearrange("p a n -> p (a n)")).then_inc(sct_ready, 1)
                dve.wait_ge(sct_ready, 1)

            def group(r, first, last):
                own = Tally(own_sem, 3 * TURNS * K * r)
                for k in range(K):
                    n = r * K + k
                    final = last and k == K - 1
                    more = not shared and not (last and k >= K - HALVES)
                    e, q = expert(r, k) + 1, (k // HALVES + 1) % 2
                    product(n, 0)
                    product(n, 1)
                    low(n, k, 0)
                    if shared:
                        select(TURNS * n, 0, own)
                    if not final:
                        split_tokens(r if k < K - 1 else r + 1, (k + 1) % K)
                    product(n, 2)
                    low(n, k, 1)
                    if shared:
                        select(TURNS * n, 1, own)
                    if not (first and k == 0):
                        result(r if k else r - 1, (k - 1) % K)
                    product(n, 3)
                    low(n, k, 2)
                    if more:
                        split_weights(e, q, 0 if k % HALVES == 0 else 2)
                    low(n, k, 3)
                    if more and k % HALVES == 0:
                        split_weights(e, q, 1)
                    if shared:
                        select(TURNS * n, 2, own)
                        for s in range(1, TURNS):
                            for part in range(3):
                                select(TURNS * n + s, part, own)
            groups(dve, group)
            result(R - 1, K - 1)
            if shared:
                assert TURNS * CHUNKS == ROUNDS
                own = Tally(own_sem, 3 * ROUNDS)
                own.wait(dve)
                own.inc(nc.vector.tensor_copy(indf[:], inds[:]))
                own.wait(dve)
                dve.wait_ge(const_in, 32)
                nc.vector.tensor_scalar(indf[:], indf[:], row0[:], None, ALU.add).then_inc(sel_ready, 1)
                dve.wait_ge(sel_full, 1)
                nc.vector.tensor_copy(WT[:].rearrange("p b e -> p (b e)"), turned[:, 0, 0:BE])
                nc.vector.tensor_copy(IX[:].rearrange("p b e -> p (b e)"), turned[:, 1, 0:BE])

        @block.tensor
        def _(pe):
            pe.wait_ge(const_in, 32 if shared else 16)
            def turn_tokens(r, k):
                n = r * K + k
                pe.wait_ge(x_in[k % 2], X_INC * (r * (K // 2) + k // 2 + 1))
                if not (isinstance(n, int) and n == 0):
                    pe.wait_ge(xl_ready, n)
                for c in range(KD):
                    for t in range(CT):
                        out = nc.tensor.transpose(turned[:, c, P * t:P * t + P], XG[k % 2][:, t, P * c:P * c + P], ident[:])
                out.then_inc(turned_full, 1)

            def up(n, k, q, f):
                i = KF * n + f
                if not (isinstance(i, int) and i < 2):
                    pe.wait_ge(hf_ready, i - 1)
                for m in range(2):
                    for c in range(KD):
                        out = three(nc, gu[f % 2][:, m, 0:N], (WH[q][m], XH[k % 2]), (WL[q][m], XL[k % 2]),
                                    (slice(None), c, slice(P * f, P * f + P)), (slice(None), c, slice(None)),
                                    c == 0, c == KD - 1)
                out.then_inc(gu_full, 1)

            def down(r, k):
                n = r * K + k
                q = (k // HALVES) % 2 if not shared else 0
                pe.wait_ge(hl_ready, KF * (n + 1))
                if not shared or (isinstance(n, int) and n == 0):
                    pe.wait_ge(wl_ready, 3 * ((expert(r, k) if not shared else 0) + 1))
                if not (isinstance(n, int) and n == 0):
                    pe.wait_ge(ys_ready, Y_INC * n)
                if shared and isinstance(n, int) and n == 0:
                    pe.wait_ge(sct_ready, 1)
                for t in range(CT):
                    for f in range(KF):
                        out = three(nc, y[:, t // 2, D * (t % 2):D * (t % 2) + D], (HH[k % 2], WH[q][2]), (HL[k % 2], WL[q][2]),
                                    (slice(None), f, slice(P * t, P * t + P)), (slice(None), f, slice(None)),
                                    f == 0, f == KF - 1)
                out.then_inc(y_full, 1)

            turn_tokens(0, 0)
            if shared:
                for t in range(TT):
                    out = nc.tensor.transpose(y[0:BE, t // 4, P * (t % 4):P * (t % 4) + P], SC[:, t, :], ident[:])
                out.then_inc(sct_full, 1)

            def group(r, first, last):
                for k in range(K):
                    n = r * K + k
                    q = (k // HALVES) % 2 if not shared else 0
                    if k % HALVES == 0 and (first or not shared):
                        pe.wait_ge(wl_ready, 3 * (expert(r, k) if not shared else 0) + 2)
                    pe.wait_ge(xl_ready, n + 1)
                    up(n, k, q, 0)
                    up(n, k, q, 1)
                    if not (last and k == K - 1):
                        turn_tokens(r if k < K - 1 else r + 1, (k + 1) % K)
                    if not (first and k == 0):
                        down(r if k else r - 1, (k - 1) % K)
                    up(n, k, q, 2)
                    up(n, k, q, 3)
            groups(pe, group)
            down(R - 1, K - 1)
            if shared:
                pe.wait_ge(sel_ready, 1)
                nc.tensor.transpose(turned[:, 0, 0:BE], vals[:], ident[0:BE, 0:BE])
                nc.tensor.transpose(turned[:, 1, 0:BE], indf[:], ident[0:BE, 0:BE]).then_inc(sel_full, 1)


def program(nc, d, B):
    with ExitStack() as ctx:
        SC = ctx.enter_context(nc.sbuf_tensor("gate_scores", [P, 1024 // P, B * E], F32))
        WT = ctx.enter_context(nc.sbuf_tensor("taken_scores", [P, B, E], F32))
        IX = ctx.enter_context(nc.sbuf_tensor("taken_rows", [P, B, E], U32))
        attention(nc, d, SC, B)
        feed_forward(nc, d, SC, WT, IX, B, True)
        feed_forward(nc, d, SC, WT, IX, B, False)


def kernel(**inputs):
    import numpy as np
    import concourse.bacc as bacc
    from concourse.bass_utils import run_bass_kernel_spmd

    a = {n.split("_", 2)[2]: np.asarray(v) for n, v in inputs.items()}
    B, T, H = a["hidden_states"].shape
    arrays = {
        "x": a["hidden_states"].reshape(B * T, H),
        **{n: a[n] for n in ("cos", "sin", "wq", "bq", "wk", "wv", "bv", "wo", "bo")},
        "gwT": a["gate_w"].T,
        "WgT": a["Wg"].transpose(0, 2, 1).reshape(E * D, F), "WuT": a["Wu"].transpose(0, 2, 1).reshape(E * D, F),
        "WdT": a["Wd"].transpose(0, 2, 1).reshape(E * F, D),
        "SgT": a["Ws_g"].T, "SuT": a["Ws_u"].T, "SdT": a["Ws_d"].T,
        "ident": np.eye(P, dtype=np.float32),
        "row0": np.repeat(np.arange(B), E)[:, None].astype(np.float32) * np.float32(T),
    }
    arrays = {n: np.ascontiguousarray(v) for n, v in arrays.items()}
    nc = bacc.Bacc("TRN2", target_bir_lowering=False, num_devices=1)
    d = {n: nc.dram_tensor(n, v.shape, mybir.dt.from_np(v.dtype), kind="ExternalInput").ap() for n, v in arrays.items()}
    d["xn2"] = nc.dram_tensor("xn2", (B * T, H), F32, kind="Internal").ap()
    d["out"] = nc.dram_tensor("out", (B * T, H), F32, kind="ExternalOutput").ap()
    program(nc, d, B)
    r = run_bass_kernel_spmd(nc, [arrays], core_ids=[0])
    return r.results[0]["out"].reshape(B, T, H)
```
